# Optimizing a Trainium2 kernel written in Bass

```python
import numpy as np
import jax
import jax.numpy as jnp

def _softmax(x, axis=-1):
    return jax.nn.softmax(x, axis=axis)

def _gelu(x):
    return jax.nn.gelu(x, approximate=True)

def _silu(x):
    return jax.nn.silu(x)

def _sigmoid(x):
    return jax.nn.sigmoid(x)

def _layernorm(x, axis=-1, eps=1e-05):
    m = jnp.mean(x, axis=axis, keepdims=True)
    v = jnp.var(x, axis=axis, keepdims=True)
    return (x - m) / jnp.sqrt(v + eps)

def _scatter_add(tgt, idx, src, axis=0):
    return tgt.at[idx].add(src)

def _segment_sum(src, seg, n):
    return jax.ops.segment_sum(src, seg, n)
kernel_name = 'mk_cond_resid_d2_seqx_r8_23d0c1'

def setup_inputs(seed: int=0):
    np.random.seed(seed)
    _w = jnp.asarray

    def _rec_inputs():
        import jax
        import jax.numpy as jnp
        _rk = jax.random.key(seed)
        x = -0.0002928 + 1 * jax.random.normal(jax.random.fold_in(_rk, 1), (2, 512, 128), jnp.float32)
        _lenS = 512 - jax.random.randint(jax.random.fold_in(_rk, 7), (2,), 0, max(1, 512 // 4) + 1, jnp.int32)
        _lenS2 = 512 - jax.random.randint(jax.random.fold_in(_rk, 8), (2,), 0, max(1, 512 // 4) + 1, jnp.int32)
        cond_256 = -0.106481 + 1.03144 * jax.random.normal(jax.random.fold_in(_rk, 11), (2, 32), jnp.float32)
        return (x, cond_256)
    x, cond_256 = _rec_inputs()

    def _L0_cond_setup():
        import jax, jax.numpy as jnp
        import numpy as np
        TOP_K = 2
        EPS = 1e-06
        B, S, H, G, E, M = (2, 256, 128, 32, 8, 256)
        key = jax.random.key(seed)
        ks = jax.random.split(key, 16)
        s_h = 1.0 / np.sqrt(H)
        s_g = 1.0 / np.sqrt(G)
        s_m = 1.0 / np.sqrt(M)
        return {'x': jax.random.normal(ks[0], (B, S, H), jnp.float32), 'genre_embed': jax.random.normal(ks[1], (B, 1, G), jnp.float32), 'rms_w': jnp.ones((H,), jnp.float32), 'wg_W': jax.random.normal(ks[2], (H, E), jnp.float32) * s_h, 'wg_b': jnp.zeros((E,), jnp.float32), 'gg_W': jax.random.normal(ks[3], (G, E), jnp.float32) * s_g, 'gg_b': jnp.zeros((E,), jnp.float32), 'W1': jax.random.normal(ks[4], (E, H, M), jnp.float32) * s_h, 'b1': jnp.zeros((E, M), jnp.float32), 'W2': jax.random.normal(ks[5], (E, M, M), jnp.float32) * s_m, 'b2': jnp.zeros((E, M), jnp.float32), 'W3': jax.random.normal(ks[6], (E, M, H), jnp.float32) * s_m, 'b3': jnp.zeros((E, H), jnp.float32)}
    _L0_cond_all = _L0_cond_setup()
    _L0_cond_in = {k: v for k, v in _L0_cond_all.items() if k in ('rms_w', 'wg_W', 'wg_b', 'gg_W', 'gg_b', 'W1', 'b1', 'W2', 'b2', 'W3', 'b3')}
    del _L0_cond_all

    def _L1_cond_setup():
        import jax, jax.numpy as jnp
        import numpy as np
        EPS = 1e-08

        def hamilton(q1, q2):
            w1, x1, y1, z1 = (q1[..., i, :] for i in range(4))
            w2, x2, y2, z2 = (q2[..., i, :] for i in range(4))
            w = w1 * w2 - x1 * x2 - y1 * y2 - z1 * z2
            x = w1 * x2 + x1 * w2 + y1 * z2 - z1 * y2
            y = w1 * y2 - x1 * z2 + y1 * w2 + z1 * x2
            z = w1 * z2 + x1 * y2 - y1 * x2 + z1 * w2
            return jnp.stack([w, x, y, z], axis=-2)

        def _normalize(q):
            return q / jnp.sqrt(jnp.sum(q * q, axis=0, keepdims=True) + EPS)
        key = jax.random.key(seed)
        k1, k2, k3, k4 = jax.random.split(key, 4)
        B, T, d_model = (4, 512, 128)
        quat_dim = d_model // 4
        x = jax.random.normal(k1, (B, T, d_model), dtype=jnp.float32)
        q_left = jax.random.normal(k2, (4, quat_dim), dtype=jnp.float32)
        q_right = jax.random.normal(k3, (4, quat_dim), dtype=jnp.float32)
        spectral_gate = jax.random.uniform(k4, (1, 1, 1, quat_dim), dtype=jnp.float32)
        return {'x': x, 'q_left': q_left, 'q_right': q_right, 'spectral_gate': spectral_gate}
    _L1_cond_all = _L1_cond_setup()
    _L1_cond_in = {k: v for k, v in _L1_cond_all.items() if k in ('q_right', 'spectral_gate')}
    del _L1_cond_all
    return {'x': x, 'cond_256': cond_256, 'L0_cond_rms_w': _L0_cond_in['rms_w'], 'L0_cond_wg_W': _L0_cond_in['wg_W'], 'L0_cond_wg_b': _L0_cond_in['wg_b'], 'L0_cond_gg_W': _L0_cond_in['gg_W'], 'L0_cond_gg_b': _L0_cond_in['gg_b'], 'L0_cond_W1': _L0_cond_in['W1'], 'L0_cond_b1': _L0_cond_in['b1'], 'L0_cond_W2': _L0_cond_in['W2'], 'L0_cond_b2': _L0_cond_in['b2'], 'L0_cond_W3': _L0_cond_in['W3'], 'L0_cond_b3': _L0_cond_in['b3'], 'L1_cond_q_right': _L1_cond_in['q_right'], 'L1_cond_spectral_gate': _L1_cond_in['spectral_gate']}

def reference(x, cond_256, L0_cond_rms_w, L0_cond_wg_W, L0_cond_wg_b, L0_cond_gg_W, L0_cond_gg_b, L0_cond_W1, L0_cond_b1, L0_cond_W2, L0_cond_b2, L0_cond_W3, L0_cond_b3, L1_cond_q_right, L1_cond_spectral_gate):
    import jax
    import jax.numpy as jnp

    def _L0_cond_ref(x, genre_embed, rms_w, wg_W, wg_b, gg_W, gg_b, W1, b1, W2, b2, W3, b3):
        import jax, jax.numpy as jnp
        import numpy as np
        TOP_K = 2
        EPS = 1e-06
        E = W1.shape[0]
        var = jnp.mean(x * x, axis=-1, keepdims=True)
        xn = rms_w * (x * jax.lax.rsqrt(var + EPS))
        gate = xn @ wg_W + wg_b + (genre_embed @ gg_W + gg_b)
        gate_w = jax.nn.softmax(gate, axis=-1)
        topk_w, topk_i = jax.lax.top_k(gate_w, TOP_K)
        cw = jnp.sum(jax.nn.one_hot(topk_i, E, dtype=x.dtype) * topk_w[..., None], axis=-2)
        h1 = jax.nn.relu(jnp.einsum('bsh,ehm->bsem', x, W1) + b1)
        h2 = jax.nn.relu(jnp.einsum('bsem,emn->bsen', h1, W2) + b2)
        out_e = jnp.einsum('bsen,enh->bseh', h2, W3) + b3
        return jnp.einsum('bseh,bse->bsh', out_e, cw)

    def _L1_cond_ref(x, q_left, q_right, spectral_gate):
        import jax, jax.numpy as jnp
        import numpy as np
        EPS = 1e-08

        def hamilton(q1, q2):
            w1, x1, y1, z1 = (q1[..., i, :] for i in range(4))
            w2, x2, y2, z2 = (q2[..., i, :] for i in range(4))
            w = w1 * w2 - x1 * x2 - y1 * y2 - z1 * z2
            x = w1 * x2 + x1 * w2 + y1 * z2 - z1 * y2
            y = w1 * y2 - x1 * z2 + y1 * w2 + z1 * x2
            z = w1 * z2 + x1 * y2 - y1 * x2 + z1 * w2
            return jnp.stack([w, x, y, z], axis=-2)

        def _normalize(q):
            return q / jnp.sqrt(jnp.sum(q * q, axis=0, keepdims=True) + EPS)
        B, T, d_model = x.shape
        quat_dim = d_model // 4
        x_quat = x.reshape(B, T, 4, quat_dim)
        x_spectral = jnp.fft.fft(x_quat, axis=1)
        x_filtered = jnp.fft.ifft(x_spectral * spectral_gate, axis=1).real.astype(x.dtype)
        q_left_n = _normalize(q_left)
        q_right_n = _normalize(q_right)
        conj_sign = jnp.array([1.0, -1.0, -1.0, -1.0], dtype=x.dtype)[:, None]
        q_right_conj = q_right_n * conj_sign
        x_right = hamilton(x_filtered, q_right_conj)
        x_rotated = hamilton(q_left_n, x_right)
        return x_rotated.reshape(B, T, d_model)
    x = x + _L0_cond_ref(x, cond_256[:, None, :], L0_cond_rms_w, L0_cond_wg_W, L0_cond_wg_b, L0_cond_gg_W, L0_cond_gg_b, L0_cond_W1, L0_cond_b1, L0_cond_W2, L0_cond_b2, L0_cond_W3, L0_cond_b3)
    x = x + _L1_cond_ref(x, cond_256, L1_cond_q_right, L1_cond_spectral_gate)
    return x

_drawn_inputs = setup_inputs


def setup_inputs(seed=0):
    import zlib

    import numpy as np

    out = dict(_drawn_inputs(seed))
    spreads = {'L0_cond_rms_w': (1.0, 0.2),
     'L0_cond_wg_b': (0.0, 0.1),
     'L0_cond_gg_b': (0.0, 0.1),
     'L0_cond_b1': (0.0, 0.346),
     'L0_cond_b2': (0.0, 0.1),
     'L0_cond_b3': (0.0, 0.1)}
    factors = {}
    for name, (base, spread) in spreads.items():
        noise = np.random.default_rng([zlib.crc32(name.encode()), seed]).standard_normal(out[name].shape)
        drawn = base * np.exp(spread * noise) if base else spread * noise
        out[name] = jnp.asarray(drawn.astype(out[name].dtype))
    for name, factor in factors.items():
        out[name] = (out[name] * factor).astype(out[name].dtype)
    return out
```

```python
from contextlib import ExitStack

import numpy as np

import concourse.bass as bass
from concourse import mybir

F32 = mybir.dt.float32
F32R = mybir.dt.float32r
ACT = mybir.ActivationFunctionType
ALU = mybir.AluOpType
AX = mybir.AxisListType

P = 128
B, S, H = 2, 512, 128
E, M, G = 8, 256, 32
MC = M // P
TB = S // P
T = B * TB
QC = 4
QD = H // QC
UNITS = E * B
RMS_EPS = 1e-6
NORM_EPS = 1e-8
BELOW_ALL = -3.0e38

W1_AT = 0
W2_AT = [M, 2 * M]
W3_AT = [3 * M, 3 * M + H]
W_COLS = 3 * M + MC * H
W_HALF = W_COLS // 2

SMALL = {}
_at = 0
for _name, _width in (("rms_w", 1), ("wg_W", E), ("q_right", QC), ("q_left", 2), ("gate", 1), ("rank", E),
                      ("right_sign", QC), ("left_sign", QC * QC), ("channel", QD), ("ident", P)):
    SMALL[_name] = (_at, _at + _width)
    _at += _width
SMALL_COLS = _at


def moe_rotate(nc, x_t, small, gate_rows, weights, biases, b3, out):
    cw_dram = nc.dram_tensor("cw_dram", [E, T * P], F32, kind="Internal").ap()

    ctx = ExitStack()
    with ctx:
        def sb(name, shape, dt=F32):
            return ctx.enter_context(nc.sbuf_tensor(name, shape, dt))

        def pb(name):
            return ctx.enter_context(nc.psum_tensor(name, [P, 512], F32))

        def sem(name):
            return ctx.enter_context(nc.semaphore(name))

        xT = sb("xT", [P, B, S])
        x_hi = sb("x_hi", [P, B, S], F32R)
        x_lo = sb("x_lo", [P, B, S], F32R)
        x_sq = sb("x_sq", [P, B, S])
        sm = sb("sm", [P, SMALL_COLS])
        gr = sb("gr", [G + 2, B + E])
        b3_sb = sb("b3_sb", [E, H])
        w_raw = [sb(f"w_raw{i}", [P, W_COLS]) for i in range(2)]
        w_hi = [sb(f"w_hi{i}", [P, W_COLS], F32R) for i in range(2)]
        w_lo = [sb(f"w_lo{i}", [P, W_COLS], F32R) for i in range(2)]
        bias = [sb(f"bias{i}", [P, 2 * MC]) for i in range(2)]
        cw_all = [sb(f"cw_all{i}", [P, T * P]) for i in range(2)]
        h1 = sb("h1", [P, MC, S])
        h1_hi = [sb(f"h1_hi{b}", [P, MC, S], F32R) for b in range(B)]
        h1_lo = [sb(f"h1_lo{b}", [P, MC, S], F32R) for b in range(B)]
        z2 = sb("z2", [P, MC, S])
        h2_hi = [sb(f"h2_hi{b}", [P, MC, S], F32R) for b in range(B)]
        h2_lo = [sb(f"h2_lo{b}", [P, MC, S], F32R) for b in range(B)]
        x1T = sb("x1T", [P, B, S])
        out_sb = sb("out_sb", [P, B, S])
        ones = sb("ones", [P, 1])
        minus_half = sb("minus_half", [P, T])
        wg_s = sb("wg_s", [P, E])
        ms = sb("ms", [P, T])
        rinv = sb("rinv", [P, T])
        logit = sb("logit", [P, T, E])
        top = sb("top", [P, T])
        below = sb("below", [P, T, E])
        prob = sb("prob", [P, T, E])
        key = sb("key", [P, T, E])
        best = sb("best", [P, T])
        first = sb("first", [P, T, E])
        rest = sb("rest", [P, T, E])
        second = sb("second", [P, T, E])
        total = sb("total", [P, T])
        scale = sb("scale", [P, T])
        cw = sb("cw", [P, E, T])
        cw_rows = sb("cw_rows", [E * T, P])
        cw_e = sb("cw_e", [E, T * P])
        q_sq = sb("q_sq", [P, QC + 2])
        q_pair = sb("q_pair", [P, 3])
        q_sum = sb("q_sum", [P, 2])
        q_norm = sb("q_norm", [P, 2])
        q_scale = sb("q_scale", [P, 1])
        right = sb("right", [P, QC])
        turned = sb("turned", [P, QC, QC])
        turned2 = sb("turned2", [P, QC, 2])
        turned1 = sb("turned1", [P, QC])
        part_a = sb("part_a", [P, QC])
        part_b = sb("part_b", [P, QC])
        coef = sb("coef", [P, QC])
        rot = sb("rot", [P, QC, QD])
        mix = sb("mix", [P, P])

        ps1 = [pb(f"ps1_{c}") for c in range(MC)]
        ps2 = [pb(f"ps2_{m}") for m in range(MC)]
        acc = [pb(f"acc{b}") for b in range(B)]
        misc = [pb(f"misc{b}") for b in range(B)]
        gate_ps = misc[0][:, 0:T * E].rearrange("p (t e) -> p t e", e=E)
        ssq_ps = misc[0][:, T * E:T * E + T]
        gbias_ps = misc[0][:, 128:128 + B * E]
        cwT_ps = misc[1][0:E * T, 0:P]

        fin = [misc[0], misc[1], ps1[0], ps1[1]]

        def small_at(name):
            a, z = SMALL[name]
            return sm[:, a:z]

        rank_bc = small_at("rank").unsqueeze(1).to_broadcast([P, T, E])
        ident = small_at("ident")

        x_in = [sem(f"x_in{b}") for b in range(B)]
        small_in = sem("small_in")
        gr_in = sem("gr_in")
        b3_in = sem("b3_in")
        raw_in = [sem(f"raw_in{i}") for i in range(2)]
        bias_in = [sem(f"bias_in{i}") for i in range(2)]
        cw_in = [sem(f"cw_in{i}") for i in range(2)]
        cw_out = sem("cw_out")
        cw_e_in = sem("cw_e_in")
        out_done = sem("out_done")
        x_sq_done = sem("x_sq_done")
        x_hi_done = sem("x_hi_done")
        x_lo_done = sem("x_lo_done")
        wg_ready = sem("wg_ready")
        gate_done = sem("gate_done")
        ms_done = sem("ms_done")
        rinv_done = sem("rinv_done")
        below_done = sem("below_done")
        prob_done = sem("prob_done")
        cw_done = sem("cw_done")
        cwT_done = sem("cwT_done")
        cw_rows_done = sem("cw_rows_done")
        w_hi_done = sem("w_hi_done")
        w_lo_done = sem("w_lo_done")
        l1_done = sem("l1_done")
        h1_act = sem("h1_act")
        h1_lo_done = sem("h1_lo_done")
        l2_done = sem("l2_done")
        z2_done = sem("z2_done")
        h2_hi_done = sem("h2_hi_done")
        h2_lo_done = sem("h2_lo_done")
        l3_done = sem("l3_done")
        mix_done = sem("mix_done")
        x1_done = sem("x1_done")
        fin_done = sem("fin_done")
        out_ready = sem("out_ready")
        dve_order = sem("dve_order")
        pool_order = sem("pool_order")

        block = ctx.enter_context(nc.Block())

        LOOPS = 3

        def unit(k, s):
            return 4 * k + s, 2 * k + s // 2, (s // 2) % 2, s % 2

        @block.sync
        def _(sp):
            sp.dma_start(sm[:, :], small).then_inc(small_in, 16)
            sp.dma_start(xT[:, 0, :], x_t[:, 0, :]).then_inc(x_in[0], 16)
            sp.dma_start(xT[:, 1, :], x_t[:, 1, :]).then_inc(x_in[1], 16)
            sp.dma_start(gr[:, :], gate_rows).then_inc(gr_in, 16)
            for e in range(2):
                sp.dma_start(bias[e][:, :], biases[e]).then_inc(bias_in[e], 16)
            sp.dma_start(w_raw[1][:, :], weights[1]).then_inc(raw_in[1], 16)
            sp.dma_start(b3_sb[:, :], b3).then_inc(b3_in, 16)
            sp.wait_ge(cw_rows_done, 1)
            sp.dma_start(cw_dram.rearrange("e (t p) -> (e t) p", p=P), cw_rows[:, :]).then_inc(cw_out, 16)
            sp.wait_ge(cw_out, 16)
            for e in range(2):
                sp.dma_start(cw_all[e][:, :], cw_dram[e:e + 1, :].to_broadcast([P, T * P])).then_inc(cw_in[e], 16)
            sp.dma_start(cw_e[:, :], cw_dram).then_inc(cw_e_in, 16)
            with sp.Fori(0, E // 2 - 1) as k:
                for i in range(2):
                    e = 2 * k + i
                    sp.wait_ge(w_lo_done, 2 * e + 2)
                    sp.dma_start(w_raw[i][:, :], weights[bass.ds(e + 2, 1), :, :].rearrange("a p c -> (a p) c")).then_inc(raw_in[i], 16)
                    sp.wait_ge(z2_done, 2 * MC * (e + 1))
                    sp.dma_start(cw_all[i][:, :], cw_dram[bass.ds(e + 2, 1), :].to_broadcast([P, T * P])).then_inc(cw_in[i], 16)
                    sp.dma_start(bias[i][:, :], biases[bass.ds(e + 2, 1), :, :].rearrange("a p c -> (a p) c")).then_inc(bias_in[i], 16)
            for b in range(B):
                rows = out[b].rearrange("(t p) h -> p t h", p=P)
                for h in range(2):
                    t = slice(h * TB // 2, (h + 1) * TB // 2)
                    sp.wait_ge(out_ready, 2 * b + h + 1)
                    sp.dma_start(rows[:, t, :], out_sb[:, b, :].rearrange("p (t h) -> p t h", h=H)[:, t, :]).then_inc(out_done, 16)
            sp.wait_ge(out_done, 16 * 2 * B)

        @block.gpsimd
        def _(pool):
            count = [0]

            def then(ins):
                ins.then_inc(pool_order, 1)
                count[0] += 1
                pool.wait_ge(pool_order, count[0])

            tt = nc.gpsimd.tensor_tensor
            nc.gpsimd.memset(ones[:, :], 1.0).then_inc(wg_ready, 1)
            then(nc.gpsimd.memset(minus_half[:, :], -0.5))
            pool.wait_ge(small_in, 16)
            nc.gpsimd.tensor_scalar(wg_s[:, :], small_at("wg_W"), small_at("rms_w"), 1.0, ALU.mult, ALU.mult).then_inc(wg_ready, 1)
            pool.wait_ge(ms_done, 1)
            tt(rinv[:, :], ms[:, :], minus_half[:, :], ALU.pow).then_inc(rinv_done, 1)

            qr, ql = small_at("q_right"), small_at("q_left")
            tt(q_sq[:, 0:QC], qr, qr, ALU.mult)
            then(tt(q_sq[:, QC:QC + 2], ql, ql, ALU.mult))
            then(tt(q_pair[:, :], q_sq[:, 0:QC + 2:2], q_sq[:, 1:QC + 2:2], ALU.add))
            tt(q_sum[:, 0:1], q_pair[:, 0:1], q_pair[:, 1:2], ALU.add)
            then(nc.gpsimd.tensor_copy(q_sum[:, 1:2], q_pair[:, 2:3]))
            then(nc.gpsimd.tensor_scalar(q_sum[:, :], q_sum[:, :], NORM_EPS, 1.0, ALU.add, ALU.mult))
            then(tt(q_norm[:, :], q_sum[:, :], minus_half[:, 0:2], ALU.pow))
            then(tt(q_scale[:, :], q_norm[:, 0:1], q_norm[:, 1:2], ALU.mult))
            then(tt(q_scale[:, :], q_scale[:, :], small_at("gate"), ALU.mult))
            then(tt(right[:, :], qr, small_at("right_sign"), ALU.mult))
            then(tt(turned[:, :, :], small_at("left_sign").rearrange("p (i k) -> p i k", k=QC),
                    right[:, :].unsqueeze(1).to_broadcast([P, QC, QC]), ALU.mult))
            then(tt(turned2[:, :, :], turned[:, :, 0:2], turned[:, :, 2:4], ALU.add))
            then(tt(turned1[:, :], turned2[:, :, 0], turned2[:, :, 1], ALU.add))
            nc.gpsimd.tensor_scalar(part_a[:, :], right[:, :], ql[:, 0:1], q_scale[:, 0:1], ALU.mult, ALU.mult)
            then(nc.gpsimd.tensor_scalar(part_b[:, :], turned1[:, :], ql[:, 1:2], q_scale[:, 0:1], ALU.mult, ALU.mult))
            then(tt(coef[:, :], part_a[:, :], part_b[:, :], ALU.add))
            then(tt(rot[:, :, :], small_at("channel").unsqueeze(1).to_broadcast([P, QC, QD]),
                    coef[:, :].unsqueeze(2).to_broadcast([P, QC, QD]), ALU.mult))
            tt(mix[:, :], rot[:, :, :].rearrange("p i d -> p (i d)"), ident, ALU.add).then_inc(mix_done, 1)

        @block.scalar
        def _(act):
            fn = nc.scalar.activation

            def split_hi(k, s, half):
                _, e, i, _ = unit(k, s)
                cols = slice(half * W_HALF, (half + 1) * W_HALF)
                act.wait_ge(raw_in[i], 16 * (k + s // 4 + 1))
                if s >= 4:
                    if half == 0:
                        act.wait_ge(l2_done, MC * B * (e - 1))
                    else:
                        act.wait_ge(l3_done, B * (e - 1))
                fn(w_hi[i][:, cols], w_raw[i][:, cols], ACT.Copy).then_inc(w_hi_done, 1)

            def layer1_out(k, s):
                u, e, i, b = unit(k, s)
                if s % 2 == 0:
                    act.wait_ge(bias_in[i], 16 * (k + s // 4 + 1))
                for c in range(MC):
                    act.wait_ge(l1_done, MC * u + c + 1)
                    if s >= 1:
                        act.wait_ge(h1_lo_done, MC * (u - 1) + c + 1)
                    fn(h1[:, c, :], ps1[c][:, :], ACT.Relu, bias=bias[i][:, c:c + 1]).then_inc(h1_act, 1)
                    if s >= 2:
                        act.wait_ge(l2_done, MC * (u - 1))
                    fn(h1_hi[b][:, c, :], ps1[c][:, :], ACT.Relu, bias=bias[i][:, c:c + 1]).then_inc(h1_act, 1)

            def layer2_out(k, s):
                u, e, i, b = unit(k, s)
                for m in range(MC):
                    act.wait_ge(z2_done, MC * u + m + 1)
                    if s >= 2:
                        act.wait_ge(l3_done, u - 1)
                    fn(h2_hi[b][:, m, :], z2[:, m, :], ACT.Relu).then_inc(h2_hi_done, 1)

            def step(k, s):
                if not (isinstance(k, int) and 4 * k + s + 1 >= UNITS):
                    layer1_out(k, s + 1)
                if not (isinstance(k, int) and 4 * k + s + 2 >= UNITS):
                    split_hi(k, (s // 2 + 1) * 2, s % 2)
                layer2_out(k, s)

            act.dma_start(w_raw[0][:, :], weights[0]).then_inc(raw_in[0], 16)
            for b in range(B):
                act.wait_ge(x_in[b], 16)
                fn(x_sq[:, b, :], xT[:, b, :], ACT.Square).then_inc(x_sq_done, 1)
                if b == 0:
                    fn(x_hi[:, b, :], xT[:, b, :], ACT.Copy).then_inc(x_hi_done, 1)
                    split_hi(0, 0, 0)
            fn(x_hi[:, 1, :], xT[:, 1, :], ACT.Copy).then_inc(x_hi_done, 1)
            split_hi(0, 0, 1)
            layer1_out(0, 0)
            act.wait_ge(below_done, 1)
            fn(prob[:, :, :], below[:, :, :], ACT.Exp).then_inc(prob_done, 1)
            act.wait_ge(cwT_done, 1)
            fn(cw_rows[:, :], cwT_ps, ACT.Copy).then_inc(cw_rows_done, 1)
            step(0, 0)
            with act.Fori(0, LOOPS) as k:
                for s in range(1, 5):
                    step(k, s)
            for s in range(1, 4):
                step(LOOPS, s)
            for b in range(B):
                for h in range(2):
                    cols = slice(h * S // 2, (h + 1) * S // 2)
                    act.wait_ge(fin_done, 2 * b + h + 1)
                    fn(out_sb[:, b, cols], fin[2 * b + h][:, 0:S // 2], ACT.Copy).then_inc(out_ready, 1)

        @block.vector
        def _(dve):
            count = [0]

            def then(ins):
                ins.then_inc(dve_order, 1)
                count[0] += 1
                dve.wait_ge(dve_order, count[0])

            tt, stt = nc.vector.tensor_tensor, nc.vector.scalar_tensor_tensor

            def bc(row):
                return row[:, :].unsqueeze(2).to_broadcast([P, T, E])

            def x_low(b):
                dve.wait_ge(x_hi_done, b + 1)
                tt(x_lo[:, b, :], xT[:, b, :], x_hi[:, b, :].bitcast(F32), ALU.subtract).then_inc(x_lo_done, 1)

            def split_lo(k, s, half):
                _, e, i, _ = unit(k, s)
                cols = slice(half * W_HALF, (half + 1) * W_HALF)
                dve.wait_ge(w_hi_done, 2 * e + half + 1)
                tt(w_lo[i][:, cols], w_raw[i][:, cols], w_hi[i][:, cols].bitcast(F32), ALU.subtract).then_inc(w_lo_done, 1)

            def layer1_low(k, s):
                u, e, i, b = unit(k, s)
                for c in range(MC):
                    dve.wait_ge(h1_act, 2 * (MC * u + c + 1))
                    tt(h1_lo[b][:, c, :], h1[:, c, :], h1_hi[b][:, c, :].bitcast(F32), ALU.subtract).then_inc(h1_lo_done, 1)

            def layer2_scale(k, s):
                u, e, i, b = unit(k, s)
                if s % 2 == 0:
                    dve.wait_ge(bias_in[i], 16 * (k + s // 4 + 1))
                    dve.wait_ge(cw_in[i], 16 * (k + s // 4 + 1))
                for m in range(MC):
                    dve.wait_ge(l2_done, MC * u + m + 1)
                    if s >= 1:
                        dve.wait_ge(h2_lo_done, MC * (u - 1) + m + 1)
                    stt(z2[:, m, :], ps2[m][:, :], bias[i][:, MC + m:MC + m + 1], cw_all[i][:, b * S:(b + 1) * S],
                        ALU.add, ALU.mult).then_inc(z2_done, 1)

            def layer2_low(k, s):
                u, e, i, b = unit(k, s)
                for m in range(MC):
                    dve.wait_ge(h2_hi_done, MC * u + m + 1)
                    stt(h2_lo[b][:, m, :], z2[:, m, :], 0.0, h2_hi[b][:, m, :].bitcast(F32),
                        ALU.max, ALU.subtract).then_inc(h2_lo_done, 1)

            def step(k, s):
                if not (isinstance(k, int) and 4 * k + s + 1 >= UNITS):
                    layer1_low(k, s + 1)
                if not (isinstance(k, int) and 4 * k + s + 2 >= UNITS):
                    split_lo(k, (s // 2 + 1) * 2, s % 2)
                layer2_scale(k, s)
                layer2_low(k, s)

            x_low(0)
            split_lo(0, 0, 0)
            dve.wait_ge(gate_done, 1)
            nc.vector.tensor_scalar(ms[:, :], ssq_ps, 1.0 / H, RMS_EPS, ALU.mult, ALU.add).then_inc(ms_done, 1)
            x_low(1)
            split_lo(0, 0, 1)
            dve.wait_ge(rinv_done, 1)
            then(tt(logit[:, :, :], gate_ps, bc(rinv), ALU.mult))
            l4 = logit[:, :, :].rearrange("p (b t) e -> p b t e", b=B)
            then(tt(l4, l4, gbias_ps.rearrange("p (b e) -> p b e", b=B).unsqueeze(2).to_broadcast([P, B, TB, E]), ALU.add))
            then(nc.vector.tensor_reduce(top[:, :], logit[:, :, :], AX.X, ALU.max))
            tt(below[:, :, :], logit[:, :, :], bc(top), ALU.subtract).then_inc(below_done, 1)
            dve.wait_ge(below_done, 1)
            then(stt(key[:, :, :], below[:, :, :], 0.0, rank_bc, ALU.is_ge, ALU.mult))
            then(nc.vector.tensor_reduce(best[:, :], key[:, :, :], AX.X, ALU.max))
            then(tt(first[:, :, :], rank_bc, bc(best), ALU.is_equal))
            then(stt(rest[:, :, :], first[:, :, :], BELOW_ALL, below[:, :, :], ALU.mult, ALU.add))
            then(nc.vector.tensor_reduce(top[:, :], rest[:, :, :], AX.X, ALU.max))
            then(tt(rest[:, :, :], rest[:, :, :], bc(top), ALU.is_equal))
            then(tt(key[:, :, :], rest[:, :, :], rank_bc, ALU.mult))
            then(nc.vector.tensor_reduce(best[:, :], key[:, :, :], AX.X, ALU.max))
            then(tt(second[:, :, :], rank_bc, bc(best), ALU.is_equal))
            then(tt(second[:, :, :], first[:, :, :], second[:, :, :], ALU.add))
            dve.wait_ge(prob_done, 1)
            then(nc.vector.tensor_reduce(total[:, :], prob[:, :, :], AX.X, ALU.add))
            then(nc.vector.reciprocal(scale[:, :], total[:, :]))
            then(tt(prob[:, :, :], prob[:, :, :], bc(scale), ALU.mult))
            tt(cw[:, :, :].rearrange("p e t -> p t e"), prob[:, :, :], second[:, :, :], ALU.mult).then_inc(cw_done, 1)
            layer1_low(0, 0)
            step(0, 0)
            with dve.Fori(0, LOOPS) as k:
                for s in range(1, 5):
                    step(k, s)
            for s in range(1, 4):
                step(LOOPS, s)
                if s >= 2:
                    b = s - 2
                    dve.wait_ge(l3_done, UNITS - B + b + 1)
                    tt(x1T[:, b, :], acc[b][:, :], xT[:, b, :], ALU.add).then_inc(x1_done, 1)

        @block.tensor
        def _(pe):
            mm = nc.tensor.matmul

            def product(out_ps, hi_w, lo_w, hi_x, lo_x, start, stop):
                mm(out_ps, hi_w, hi_x, start=start, stop=False)
                mm(out_ps, hi_w, lo_x, start=False, stop=False)
                return mm(out_ps, lo_w, hi_x, start=False, stop=stop)

            def layer1(k, s):
                u, e, i, b = unit(k, s)
                if s % 2 == 0:
                    pe.wait_ge(w_lo_done, 2 * e + 1)
                for c in range(MC):
                    if s >= 1:
                        pe.wait_ge(h1_act, 2 * (MC * (u - 1) + c + 1))
                    w = slice(W1_AT + c * P, W1_AT + (c + 1) * P)
                    product(ps1[c][:, :], w_hi[i][:, w], w_lo[i][:, w], x_hi[:, b, :], x_lo[:, b, :],
                            True, True).then_inc(l1_done, 1)

            def layer2(k, s):
                u, e, i, b = unit(k, s)
                if s % 2 == 0:
                    pe.wait_ge(w_lo_done, 2 * e + 2)
                pe.wait_ge(h1_lo_done, MC * (u + 1))
                for m in range(MC):
                    if s >= 1:
                        pe.wait_ge(z2_done, MC * (u - 1) + m + 1)
                    for c in range(MC):
                        w = slice(W2_AT[c] + m * P, W2_AT[c] + (m + 1) * P)
                        last = product(ps2[m][:, :], w_hi[i][:, w], w_lo[i][:, w], h1_hi[b][:, c, :],
                                       h1_lo[b][:, c, :], c == 0, c == MC - 1)
                    last.then_inc(l2_done, 1)

            def layer3(k, s):
                u, e, i, b = unit(k, s)
                final = isinstance(k, int) and 4 * k + s >= UNITS - B
                for c in range(MC):
                    pe.wait_ge(h2_lo_done, MC * u + c + 1)
                    w = slice(W3_AT[c], W3_AT[c] + H)
                    last = product(acc[b][:, :], w_hi[i][:, w], w_lo[i][:, w], h2_hi[b][:, c, :],
                                   h2_lo[b][:, c, :], False, final and c == MC - 1)
                last.then_inc(l3_done, 1)

            def finish(b):
                pe.wait_ge(x1_done, b + 1)
                for t in range(TB):
                    cols = slice(t * P, (t + 1) * P)
                    half = t // (TB // 2)
                    at = t % (TB // 2) * P
                    last = mm(fin[2 * b + half][:, at:at + P], x1T[:, b, cols], mix[:, :], start=True, stop=True)
                    if t % (TB // 2) == TB // 2 - 1:
                        last.then_inc(fin_done, 1)

            pe.wait_ge(wg_ready, 2)
            pe.wait_ge(gr_in, 16)
            for b in range(B):
                mm(gbias_ps[:, b * E:(b + 1) * E], gr[:, b:b + 1].to_broadcast([G + 2, P]), gr[:, B:B + E], start=True, stop=True)
            for b in range(B):
                pe.wait_ge(x_in[b], 16)
                pe.wait_ge(x_sq_done, b + 1)
                for t in range(TB):
                    cols = slice(t * P, (t + 1) * P)
                    n = b * TB + t
                    mm(gate_ps[:, n, :], xT[:, b, cols], wg_s[:, :], start=True, stop=True)
                    last = mm(ssq_ps[:, n:n + 1], x_sq[:, b, cols], ones[:, :], start=True, stop=True)
            last.then_inc(gate_done, 1)
            pe.wait_ge(x_lo_done, 1)
            layer1(0, 0)
            pe.wait_ge(cw_done, 1)
            nc.tensor.transpose(cwT_ps, cw[:, :, :].rearrange("p e t -> p (e t)"), ident).then_inc(cwT_done, 1)
            pe.wait_ge(x_lo_done, 2)
            layer1(0, 1)
            layer2(0, 0)
            pe.wait_ge(b3_in, 16)
            pe.wait_ge(cw_e_in, 16)
            for b in range(B):
                mm(acc[b][:, :], b3_sb[:, :], cw_e[:, b * S:(b + 1) * S], start=True, stop=False)
            with pe.Fori(0, LOOPS) as k:
                for s in range(1, 5):
                    layer1(k, s + 1)
                    layer2(k, s)
                    layer3(k, s - 1)
            layer1(LOOPS, 2)
            layer2(LOOPS, 1)
            layer3(LOOPS, 0)
            layer1(LOOPS, 3)
            layer2(LOOPS, 2)
            layer3(LOOPS, 1)
            layer2(LOOPS, 3)
            pe.wait_ge(mix_done, 1)
            layer3(LOOPS, 2)
            finish(0)
            layer3(LOOPS, 3)
            pe.wait_ge(h1_act, 2 * MC * UNITS)
            finish(1)



def _small_operands(a):
    j = np.arange(P) // QD
    d = np.arange(P) % QD
    k = np.arange(QC)
    right = np.array([[1, 1, 1, 1], [-1, 1, -1, 1], [-1, 1, 1, -1], [-1, -1, 1, 1]])
    left = np.array([[0, -1, -1, -1], [1, 0, -1, 1], [1, 1, 0, -1], [1, -1, 1, 0]])
    parts = {
        "rms_w": a["L0_cond_rms_w"].reshape(P, 1),
        "wg_W": a["L0_cond_wg_W"],
        "q_right": a["L1_cond_q_right"][k[None, :] ^ j[:, None], d[:, None]],
        "q_left": a["cond_256"][:, d].T,
        "gate": a["L1_cond_spectral_gate"].reshape(QD)[d].reshape(P, 1),
        "rank": np.broadcast_to(np.arange(E, 0, -1), (P, E)),
        "right_sign": right[:, j].T,
        "left_sign": np.broadcast_to(left.reshape(1, -1), (P, QC * QC)),
        "channel": d[:, None] == np.arange(QD)[None, :],
        "ident": np.eye(P),
    }
    out = np.empty((P, SMALL_COLS), np.float32)
    for name, (lo, hi) in SMALL.items():
        out[:, lo:hi] = parts[name]
    return out


def kernel(**inputs):
    import concourse.bacc as _bacc
    from concourse.bass_utils import run_bass_kernel_spmd as _run

    a = {name: np.asarray(v) for name, v in inputs.items()}
    weights = np.empty((E, P, W_COLS), np.float32)
    weights[:, :, W1_AT:W1_AT + M] = a["L0_cond_W1"]
    for c in range(MC):
        weights[:, :, W2_AT[c]:W2_AT[c] + M] = a["L0_cond_W2"][:, c * P:(c + 1) * P]
        weights[:, :, W3_AT[c]:W3_AT[c] + H] = a["L0_cond_W3"][:, c * P:(c + 1) * P]
    biases = np.stack([a["L0_cond_b1"].reshape(E, MC, P), a["L0_cond_b2"].reshape(E, MC, P)], axis=1)
    gate_rows = np.ones((G + 2, B + E), np.float32)
    gate_rows[0:G, 0:B] = a["cond_256"].T
    gate_rows[0:G, B:] = a["L0_cond_gg_W"]
    gate_rows[G, B:] = a["L0_cond_wg_b"]
    gate_rows[G + 1, B:] = a["L0_cond_gg_b"]
    arrays = {
        "x_t": np.ascontiguousarray(a["x"].transpose(2, 0, 1)),
        "small": _small_operands(a),
        "gate_rows": gate_rows,
        "weights": weights,
        "biases": np.ascontiguousarray(biases.reshape(E, 2 * MC, P).transpose(0, 2, 1)),
        "b3": np.ascontiguousarray(a["L0_cond_b3"]),
    }
    nc = _bacc.Bacc("TRN2", target_bir_lowering=False, num_devices=1)
    args = [nc.dram_tensor(name, v.shape, F32, kind="ExternalInput").ap() for name, v in arrays.items()]
    out = nc.dram_tensor("out", (B, S, H), F32, kind="ExternalOutput").ap()
    moe_rotate(nc, *args, out)
    r = _run(nc, [arrays], core_ids=[0])
    return r.results[0]["out"]
```

```python
from contextlib import ExitStack

import numpy as np

import concourse.bass as bass
from concourse import mybir

F32 = mybir.dt.float32
F32R = mybir.dt.float32r
ACT = mybir.ActivationFunctionType
ALU = mybir.AluOpType
AX = mybir.AxisListType

P = 128
B, S, H = 2, 512, 128
E, M, G = 8, 256, 32
MC = M // P
TB = S // P
T = B * TB
QC = 4
QD = H // QC
UNITS = E * B
STACK = (0, 32, 64)
RMS_EPS = 1e-6
NORM_EPS = 1e-8
BELOW_ALL = -3.0e38

W1_AT = 0
W2_AT = [M, 2 * M]
W3_AT = [3 * M, 3 * M + H]
W_COLS = 3 * M + MC * H
W_HALF = W_COLS // 2

SMALL = {}
_at = 0
for _name, _width in (("rms_w", 1), ("wg_W", E), ("q_right", QC), ("q_left", 2), ("gate", 1), ("rank", E),
                      ("right_sign", QC), ("left_sign", QC * QC), ("channel", QD), ("ident", P)):
    SMALL[_name] = (_at, _at + _width)
    _at += _width
SMALL_COLS = _at


def moe_rotate(nc, x, x_t, small, gate_rows, weights, biases, b3, out):
    cw_dram = nc.dram_tensor("cw_dram", [E, T * P], F32, kind="Internal").ap()

    ctx = ExitStack()
    with ctx:
        def sb(name, shape, dt=F32):
            return ctx.enter_context(nc.sbuf_tensor(name, shape, dt))

        def pb(name):
            return ctx.enter_context(nc.psum_tensor(name, [P, 512], F32))

        def sem(name):
            return ctx.enter_context(nc.semaphore(name))

        xT = sb("xT", [P, B, S])
        x_hi = sb("x_hi", [P, B, S], F32R)
        x_lo = sb("x_lo", [P, B, S], F32R)
        x_tok = sb("x_tok", [P, T, H])
        x_sq = sb("x_sq", [P, T, H])
        ident_r = sb("ident_r", [P, P], F32R)
        sm = sb("sm", [P, SMALL_COLS])
        gr = sb("gr", [G + 2, B + E])
        b3_raw = sb("b3_raw", [P, H])
        b3_parts = sb("b3_parts", [P, H], F32R)
        cw_raw = sb("cw_raw", [P, T * P])
        cw_parts = sb("cw_parts", [P, T * P], F32R)
        w_raw = [sb(f"w_raw{i}", [P, W_COLS]) for i in range(2)]
        w_hi = [sb(f"w_hi{i}", [P, W_COLS], F32R) for i in range(2)]
        w_lo = [sb(f"w_lo{i}", [P, W_COLS], F32R) for i in range(2)]
        bias = [sb(f"bias{i}", [P, 2 * MC]) for i in range(2)]
        cw_all = [sb(f"cw_all{i}", [P, T * P]) for i in range(2)]
        h1 = sb("h1", [P, MC, S])
        h1_hi = [sb(f"h1_hi{b}", [P, MC, S], F32R) for b in range(B)]
        h1_lo = [sb(f"h1_lo{b}", [P, MC, S], F32R) for b in range(B)]
        z2 = sb("z2", [P, MC, S])
        h2_hi = [sb(f"h2_hi{b}", [P, MC, S], F32R) for b in range(B)]
        h2_lo = [sb(f"h2_lo{b}", [P, MC, S], F32R) for b in range(B)]
        x1T = sb("x1T", [P, B, S])
        out_sb = sb("out_sb", [P, B, S])
        minus_half = sb("minus_half", [P, T])
        wg_s = sb("wg_s", [P, E])
        ssq = sb("ssq", [P, T])
        ms = sb("ms", [P, T])
        rinv = sb("rinv", [P, T])
        logit = sb("logit", [P, T, E])
        top = sb("top", [P, T])
        below = sb("below", [P, T, E])
        prob = sb("prob", [P, T, E])
        key = sb("key", [P, T, E])
        best = sb("best", [P, T])
        first = sb("first", [P, T, E])
        rest = sb("rest", [P, T, E])
        second = sb("second", [P, T, E])
        total = sb("total", [P, T])
        scale = sb("scale", [P, T])
        cw = sb("cw", [P, E, T])
        cw_rows = sb("cw_rows", [E * T, P])
        q_sq = sb("q_sq", [P, QC + 2])
        q_pair = sb("q_pair", [P, 3])
        q_sum = sb("q_sum", [P, 2])
        q_norm = sb("q_norm", [P, 2])
        q_scale = sb("q_scale", [P, 1])
        right = sb("right", [P, QC])
        turned = sb("turned", [P, QC, QC])
        turned2 = sb("turned2", [P, QC, 2])
        turned1 = sb("turned1", [P, QC])
        part_a = sb("part_a", [P, QC])
        part_b = sb("part_b", [P, QC])
        coef = sb("coef", [P, QC])
        rot = sb("rot", [P, QC, QD])
        mix = sb("mix", [P, P])

        ps1 = [pb(f"ps1_{c}") for c in range(MC)]
        ps2 = [[pb(f"ps2_{b}_{m}") for m in range(MC)] for b in range(B)]
        acc = [pb(f"acc{b}") for b in range(B)]
        gate_ps = acc[0][:, 0:T * E].rearrange("p (t e) -> p t e", e=E)
        gbias_ps = acc[0][:, T * E:T * E + B * E]
        cwT_ps = acc[1][0:E * T, 0:P]
        fin = [ps1[0], ps1[1], ps2[0][0], ps2[0][1]]

        def small_at(name):
            a, z = SMALL[name]
            return sm[:, a:z]

        rank_bc = small_at("rank").unsqueeze(1).to_broadcast([P, T, E])
        ident = small_at("ident")

        x_in = [sem(f"x_in{b}") for b in range(B)]
        x_tok_in = sem("x_tok_in")
        raw_half_in = sem("raw_half_in")
        cw_half_in = sem("cw_half_in")
        small_in = sem("small_in")
        gr_in = sem("gr_in")
        b3_in = sem("b3_in")
        raw_in = [sem(f"raw_in{i}") for i in range(2)]
        bias_in = [sem(f"bias_in{i}") for i in range(2)]
        cw_in = [sem(f"cw_in{i}") for i in range(2)]
        cw_out = sem("cw_out")
        cw_raw_in = sem("cw_raw_in")
        bias3_done = sem("bias3_done")
        out_done = sem("out_done")
        x_sq_done = sem("x_sq_done")
        ssq_done = sem("ssq_done")
        ident_done = sem("ident_done")
        zeroed = sem("zeroed")
        x_hi_done = sem("x_hi_done")
        x_lo_done = sem("x_lo_done")
        wg_ready = sem("wg_ready")
        gate_done = sem("gate_done")
        ms_done = sem("ms_done")
        rinv_done = sem("rinv_done")
        below_done = sem("below_done")
        prob_done = sem("prob_done")
        cw_done = sem("cw_done")
        cwT_done = sem("cwT_done")
        cw_rows_done = sem("cw_rows_done")
        w_hi_done = sem("w_hi_done")
        w_lo_done = sem("w_lo_done")
        l1_done = sem("l1_done")
        h1_act = sem("h1_act")
        h1_lo_done = sem("h1_lo_done")
        l2_done = sem("l2_done")
        z2_done = sem("z2_done")
        h2_hi_done = sem("h2_hi_done")
        h2_lo_done = sem("h2_lo_done")
        l3_done = sem("l3_done")
        mix_done = sem("mix_done")
        x1_done = sem("x1_done")
        fin_done = sem("fin_done")
        out_ready = sem("out_ready")
        dve_order = sem("dve_order")
        pool_order = sem("pool_order")

        block = ctx.enter_context(nc.Block())

        LOOPS = 3

        def unit(k, s):
            return 4 * k + s, 2 * k + s // 2, (s // 2) % 2, s % 2

        @block.sync
        def _(sp):
            sp.dma_start(sm[:, :], small).then_inc(small_in, 16)
            sp.dma_start(xT[:, 0, :], x_t[:, 0, :]).then_inc(x_in[0], 16)
            sp.dma_start(xT[:, 1, :], x_t[:, 1, :]).then_inc(x_in[1], 16)
            sp.dma_start(w_raw[0][:, W_HALF:], weights[0, :, W_HALF:]).then_inc(raw_in[0], 16)
            for e in range(2):
                sp.dma_start(bias[e][:, :], biases[e]).then_inc(bias_in[e], 16)
            sp.dma_start(w_raw[1][:, :], weights[1]).then_inc(raw_in[1], 16)
            sp.wait_ge(zeroed, 2)
            for row in STACK:
                sp.dma_start(b3_raw[row:row + E, :], b3).then_inc(b3_in, 16)
            sp.wait_ge(cw_rows_done, 1)
            sp.dma_start(cw_dram.rearrange("e (t p) -> (e t) p", p=P), cw_rows[:, :]).then_inc(cw_out, 16)
            sp.wait_ge(cw_out, 16)
            sp.dma_start(cw_all[0][:, 0:S], cw_dram[0:1, 0:S].to_broadcast([P, S])).then_inc(cw_half_in, 16)
            sp.dma_start(cw_all[0][:, S:], cw_dram[0:1, S:].to_broadcast([P, S])).then_inc(cw_in[0], 16)
            sp.dma_start(cw_all[1][:, :], cw_dram[1:2, :].to_broadcast([P, T * P])).then_inc(cw_in[1], 16)
            for row in STACK:
                sp.dma_start(cw_raw[row:row + E, :], cw_dram).then_inc(cw_raw_in, 16)
            with sp.Fori(0, E // 2 - 1) as k:
                for i in range(2):
                    e = 2 * k + i
                    sp.wait_ge(w_lo_done, 2 * e + 2)
                    sp.dma_start(w_raw[i][:, :], weights[bass.ds(e + 2, 1), :, :].rearrange("a p c -> (a p) c")).then_inc(raw_in[i], 16)
                    sp.wait_ge(z2_done, 2 * MC * (e + 1))
                    sp.dma_start(cw_all[i][:, :], cw_dram[bass.ds(e + 2, 1), :].to_broadcast([P, T * P])).then_inc(cw_in[i], 16)
                    sp.dma_start(bias[i][:, :], biases[bass.ds(e + 2, 1), :, :].rearrange("a p c -> (a p) c")).then_inc(bias_in[i], 16)
            for b in range(B):
                rows = out[b].rearrange("(t p) h -> p t h", p=P)
                for h in range(2):
                    t = slice(h * TB // 2, (h + 1) * TB // 2)
                    sp.wait_ge(out_ready, 2 * b + h + 1)
                    sp.dma_start(rows[:, t, :], out_sb[:, b, :].rearrange("p (t h) -> p t h", h=H)[:, t, :]).then_inc(out_done, 16)
            sp.wait_ge(out_done, 16 * 2 * B)

        @block.gpsimd
        def _(pool):
            count = [0]

            def then(ins):
                ins.then_inc(pool_order, 1)
                count[0] += 1
                pool.wait_ge(pool_order, count[0])

            tt = nc.gpsimd.tensor_tensor
            then(nc.gpsimd.memset(minus_half[:, :], -0.5))
            nc.gpsimd.memset(b3_raw[:, :], 0.0).then_inc(zeroed, 1)
            nc.gpsimd.memset(cw_raw[:, :], 0.0).then_inc(zeroed, 1)
            pool.wait_ge(small_in, 16)
            nc.gpsimd.tensor_scalar(wg_s[:, :], small_at("wg_W"), small_at("rms_w"), 1.0, ALU.mult, ALU.mult).then_inc(wg_ready, 1)
            nc.gpsimd.tensor_copy(ident_r[:, :], ident).then_inc(ident_done, 1)
            pool.wait_ge(ms_done, 1)
            tt(rinv[:, :], ms[:, :], minus_half[:, :], ALU.pow).then_inc(rinv_done, 1)

            qr, ql = small_at("q_right"), small_at("q_left")
            tt(q_sq[:, 0:QC], qr, qr, ALU.mult)
            then(tt(q_sq[:, QC:QC + 2], ql, ql, ALU.mult))
            then(tt(q_pair[:, :], q_sq[:, 0:QC + 2:2], q_sq[:, 1:QC + 2:2], ALU.add))
            tt(q_sum[:, 0:1], q_pair[:, 0:1], q_pair[:, 1:2], ALU.add)
            then(nc.gpsimd.tensor_copy(q_sum[:, 1:2], q_pair[:, 2:3]))
            then(nc.gpsimd.tensor_scalar(q_sum[:, :], q_sum[:, :], NORM_EPS, 1.0, ALU.add, ALU.mult))
            then(tt(q_norm[:, :], q_sum[:, :], minus_half[:, 0:2], ALU.pow))
            then(tt(q_scale[:, :], q_norm[:, 0:1], q_norm[:, 1:2], ALU.mult))
            then(tt(q_scale[:, :], q_scale[:, :], small_at("gate"), ALU.mult))
            then(tt(right[:, :], qr, small_at("right_sign"), ALU.mult))
            then(tt(turned[:, :, :], small_at("left_sign").rearrange("p (i k) -> p i k", k=QC),
                    right[:, :].unsqueeze(1).to_broadcast([P, QC, QC]), ALU.mult))
            then(tt(turned2[:, :, :], turned[:, :, 0:2], turned[:, :, 2:4], ALU.add))
            then(tt(turned1[:, :], turned2[:, :, 0], turned2[:, :, 1], ALU.add))
            nc.gpsimd.tensor_scalar(part_a[:, :], right[:, :], ql[:, 0:1], q_scale[:, 0:1], ALU.mult, ALU.mult)
            then(nc.gpsimd.tensor_scalar(part_b[:, :], turned1[:, :], ql[:, 1:2], q_scale[:, 0:1], ALU.mult, ALU.mult))
            then(tt(coef[:, :], part_a[:, :], part_b[:, :], ALU.add))
            then(tt(rot[:, :, :], small_at("channel").unsqueeze(1).to_broadcast([P, QC, QD]),
                    coef[:, :].unsqueeze(2).to_broadcast([P, QC, QD]), ALU.mult))
            tt(mix[:, :], rot[:, :, :].rearrange("p i d -> p (i d)"), ident, ALU.add).then_inc(mix_done, 1)

            lo_b3, lo_cw = slice(STACK[1], STACK[1] + E), slice(STACK[2], STACK[2] + E)
            pool.wait_ge(b3_in, 16 * len(STACK))
            then(nc.gpsimd.tensor_copy(b3_parts[:, :], b3_raw[:, :]))
            tt(b3_parts[lo_b3, :], b3_raw[lo_b3, :], b3_parts[lo_b3, :].bitcast(F32), ALU.subtract).then_inc(bias3_done, 1)
            pool.wait_ge(cw_raw_in, 16 * len(STACK))
            for b in range(B):
                cols = slice(b * S, (b + 1) * S)
                pool.wait_ge(bias3_done, b + 1)
                then(nc.gpsimd.tensor_copy(cw_parts[:, cols], cw_raw[:, cols]))
                tt(cw_parts[lo_cw, cols], cw_raw[lo_cw, cols], cw_parts[lo_cw, cols].bitcast(F32), ALU.subtract).then_inc(bias3_done, 1)

        @block.scalar
        def _(act):
            fn = nc.scalar.activation

            def split_hi(k, s, half):
                _, e, i, _ = unit(k, s)
                cols = slice(half * W_HALF, (half + 1) * W_HALF)
                if half == 0 and s == 0:
                    act.wait_ge(raw_half_in, 16)
                else:
                    act.wait_ge(raw_in[i], 16 * (k + s // 4 + 1))
                if half == 0 and s >= 4:
                    act.wait_ge(l2_done, MC * B * (e - 1))
                if half == 1 and s >= 2:
                    act.wait_ge(l1_done, MC * B * e + 1)
                fn(w_hi[i][:, cols], w_raw[i][:, cols], ACT.Copy).then_inc(w_hi_done, 1)

            def layer1_out(k, s):
                u, e, i, b = unit(k, s)
                if s % 2 == 0:
                    act.wait_ge(bias_in[i], 16 * (k + s // 4 + 1))
                for c in range(MC):
                    act.wait_ge(l1_done, MC * u + c + 1)
                    if s >= 1:
                        act.wait_ge(h1_lo_done, MC * (u - 1) + c + 1)
                    fn(h1[:, c, :], ps1[c][:, :], ACT.Relu, bias=bias[i][:, c:c + 1]).then_inc(h1_act, 1)
                    if s >= 2:
                        act.wait_ge(l2_done, MC * (u - 1))
                    fn(h1_hi[b][:, c, :], ps1[c][:, :], ACT.Relu, bias=bias[i][:, c:c + 1]).then_inc(h1_act, 1)

            def layer2_out(k, s):
                u, e, i, b = unit(k, s)
                if s >= 2:
                    act.wait_ge(l3_done, u - 1)
                for m in range(MC):
                    act.wait_ge(z2_done, MC * u + m + 1)
                    fn(h2_hi[b][:, m, :], z2[:, m, :], ACT.Relu).then_inc(h2_hi_done, 1)

            def step(k, s):
                split = not (isinstance(k, int) and 4 * k + s + 2 >= UNITS)
                if split and s % 2 == 0:
                    split_hi(k, s + 2, 0)
                if not (isinstance(k, int) and 4 * k + s + 1 >= UNITS):
                    layer1_out(k, s + 1)
                if split and s % 2 == 1:
                    split_hi(k, s + 1, 1)
                layer2_out(k, s)

            act.dma_start(x_tok[:, :, :], x.rearrange("b (t p) h -> p (b t) h", p=P)).then_inc(x_tok_in, 16)
            act.dma_start(gr[:, :], gate_rows).then_inc(gr_in, 16)
            act.dma_start(w_raw[0][:, 0:W_HALF], weights[0, :, 0:W_HALF]).then_inc(raw_half_in, 16)
            act.wait_ge(x_tok_in, 16)
            for b in range(B):
                fn(x_sq[:, b * TB:(b + 1) * TB, :], x_tok[:, b * TB:(b + 1) * TB, :], ACT.Square).then_inc(x_sq_done, 1)
            act.wait_ge(x_in[0], 16)
            fn(x_hi[:, 0, :], xT[:, 0, :], ACT.Copy).then_inc(x_hi_done, 1)
            split_hi(0, 0, 0)
            act.wait_ge(x_in[1], 16)
            fn(x_hi[:, 1, :], xT[:, 1, :], ACT.Copy).then_inc(x_hi_done, 1)
            split_hi(0, 0, 1)
            act.wait_ge(below_done, 1)
            fn(prob[:, :, :], below[:, :, :], ACT.Exp).then_inc(prob_done, 1)
            layer1_out(0, 0)
            act.wait_ge(cwT_done, 1)
            fn(cw_rows[:, :], cwT_ps, ACT.Copy).then_inc(cw_rows_done, 1)
            step(0, 0)
            with act.Fori(0, LOOPS) as k:
                for s in range(1, 5):
                    step(k, s)
            for s in range(1, 4):
                step(LOOPS, s)
            act.wait_ge(l3_done, UNITS - 1)
            fn(x1T[:, 0, :], acc[0][:, :], ACT.Copy).then_inc(x1_done, 2)
            act.wait_ge(l3_done, UNITS)
            for h in range(2):
                cols = slice(h * S // 2, (h + 1) * S // 2)
                fn(x1T[:, 1, cols], acc[1][:, cols], ACT.Copy).then_inc(x1_done, 1)
            for b in range(B):
                for h in range(2):
                    cols = slice(h * S // 2, (h + 1) * S // 2)
                    act.wait_ge(fin_done, 2 * b + h + 1)
                    fn(out_sb[:, b, cols], fin[2 * b + h][:, 0:S // 2], ACT.Copy).then_inc(out_ready, 1)

        @block.vector
        def _(dve):
            count = [0]

            def then(ins):
                ins.then_inc(dve_order, 1)
                count[0] += 1
                dve.wait_ge(dve_order, count[0])

            tt, stt = nc.vector.tensor_tensor, nc.vector.scalar_tensor_tensor

            def bc(row):
                return row[:, :].unsqueeze(2).to_broadcast([P, T, E])

            def x_low(b):
                dve.wait_ge(x_hi_done, b + 1)
                tt(x_lo[:, b, :], xT[:, b, :], x_hi[:, b, :].bitcast(F32), ALU.subtract).then_inc(x_lo_done, 1)

            def split_lo(k, s, half):
                _, e, i, _ = unit(k, s)
                cols = slice(half * W_HALF, (half + 1) * W_HALF)
                dve.wait_ge(w_hi_done, 2 * e + half + 1)
                tt(w_lo[i][:, cols], w_raw[i][:, cols], w_hi[i][:, cols].bitcast(F32), ALU.subtract).then_inc(w_lo_done, 1)

            def layer1_low(k, s, c):
                u, e, i, b = unit(k, s)
                dve.wait_ge(h1_act, 2 * (MC * u + c + 1))
                tt(h1_lo[b][:, c, :], h1[:, c, :], h1_hi[b][:, c, :].bitcast(F32), ALU.subtract).then_inc(h1_lo_done, 1)

            def layer2_scale(k, s, m):
                u, e, i, b = unit(k, s)
                if m == 0:
                    if s % 2 == 0:
                        dve.wait_ge(bias_in[i], 16 * (k + s // 4 + 1))
                    if s == 0:
                        dve.wait_ge(cw_half_in, 16)
                    else:
                        dve.wait_ge(cw_in[i], 16 * (k + s // 4 + 1))
                dve.wait_ge(l2_done, MC * u + m + 1)
                if s >= 1:
                    dve.wait_ge(h2_lo_done, MC * u)
                stt(z2[:, m, :], ps2[b][m][:, :], bias[i][:, MC + m:MC + m + 1], cw_all[i][:, b * S:(b + 1) * S],
                    ALU.add, ALU.mult).then_inc(z2_done, 1)

            def layer2_low(k, s, m, n):
                u, e, i, b = unit(k, s)
                dve.wait_ge(h2_hi_done, MC * u + m + n)
                stt(h2_lo[b][:, m:m + n, :], z2[:, m:m + n, :], 0.0, h2_hi[b][:, m:m + n, :].bitcast(F32),
                    ALU.max, ALU.subtract).then_inc(h2_lo_done, n)

            def step(k, s):
                for c in range(MC):
                    if not (isinstance(k, int) and 4 * k + s + 1 >= UNITS):
                        layer1_low(k, s + 1, c)
                    layer2_scale(k, s, c)
                if not (isinstance(k, int) and 4 * k + s + 2 >= UNITS):
                    split_lo(k, (s // 2 + 1) * 2, s % 2)
                layer2_low(k, s, 0, MC)

            for b in range(B):
                dve.wait_ge(x_sq_done, b + 1)
                nc.vector.tensor_reduce(ssq[:, b * TB:(b + 1) * TB], x_sq[:, b * TB:(b + 1) * TB, :], AX.X, ALU.add).then_inc(ssq_done, 1)
            dve.wait_ge(ssq_done, B)
            nc.vector.tensor_scalar(ms[:, :], ssq[:, :], 1.0 / H, RMS_EPS, ALU.mult, ALU.add).then_inc(ms_done, 1)
            x_low(0)
            split_lo(0, 0, 0)
            x_low(1)
            dve.wait_ge(gate_done, 1)
            dve.wait_ge(rinv_done, 1)
            then(tt(logit[:, :, :], gate_ps, bc(rinv), ALU.mult))
            l4 = logit[:, :, :].rearrange("p (b t) e -> p b t e", b=B)
            then(tt(l4, l4, gbias_ps.rearrange("p (b e) -> p b e", b=B).unsqueeze(2).to_broadcast([P, B, TB, E]), ALU.add))
            then(nc.vector.tensor_reduce(top[:, :], logit[:, :, :], AX.X, ALU.max))
            tt(below[:, :, :], logit[:, :, :], bc(top), ALU.subtract).then_inc(below_done, 1)
            dve.wait_ge(below_done, 1)
            then(stt(key[:, :, :], below[:, :, :], 0.0, rank_bc, ALU.is_ge, ALU.mult))
            then(nc.vector.tensor_reduce(best[:, :], key[:, :, :], AX.X, ALU.max))
            then(tt(first[:, :, :], rank_bc, bc(best), ALU.is_equal))
            then(stt(rest[:, :, :], first[:, :, :], BELOW_ALL, below[:, :, :], ALU.mult, ALU.add))
            then(nc.vector.tensor_reduce(top[:, :], rest[:, :, :], AX.X, ALU.max))
            then(tt(rest[:, :, :], rest[:, :, :], bc(top), ALU.is_equal))
            then(tt(key[:, :, :], rest[:, :, :], rank_bc, ALU.mult))
            then(nc.vector.tensor_reduce(best[:, :], key[:, :, :], AX.X, ALU.max))
            then(tt(second[:, :, :], rank_bc, bc(best), ALU.is_equal))
            then(tt(second[:, :, :], first[:, :, :], second[:, :, :], ALU.add))
            dve.wait_ge(prob_done, 1)
            then(nc.vector.tensor_reduce(total[:, :], prob[:, :, :], AX.X, ALU.add))
            then(nc.vector.reciprocal(scale[:, :], total[:, :]))
            then(tt(prob[:, :, :], prob[:, :, :], bc(scale), ALU.mult))
            tt(cw[:, :, :].rearrange("p e t -> p t e"), prob[:, :, :], second[:, :, :], ALU.mult).then_inc(cw_done, 1)
            layer1_low(0, 0, 0)
            layer1_low(0, 0, 1)
            split_lo(0, 0, 1)
            layer1_low(0, 1, 0)
            layer1_low(0, 1, 1)
            split_lo(0, 2, 0)
            for m in range(MC):
                layer2_scale(0, 0, m)
            for m in range(MC):
                layer2_low(0, 0, m, 1)
            with dve.Fori(0, LOOPS) as k:
                for s in range(1, 5):
                    step(k, s)
            step(LOOPS, 1)
            step(LOOPS, 2)
            for m in range(MC):
                layer2_scale(LOOPS, 3, m)
            for m in range(MC):
                layer2_low(LOOPS, 3, m, 1)

        @block.tensor
        def _(pe):
            mm = nc.tensor.matmul

            def product(out_ps, hi_w, lo_w, hi_x, lo_x, start, stop):
                mm(out_ps, hi_w, hi_x, start=start, stop=False)
                mm(out_ps, hi_w, lo_x, start=False, stop=False)
                return mm(out_ps, lo_w, hi_x, start=False, stop=stop)

            def layer1(k, s):
                u, e, i, b = unit(k, s)
                if s % 2 == 0:
                    pe.wait_ge(w_lo_done, 2 * e + 1)
                for c in range(MC):
                    if s >= 1:
                        pe.wait_ge(h1_act, 2 * (MC * (u - 1) + c + 1))
                    w = slice(W1_AT + c * P, W1_AT + (c + 1) * P)
                    product(ps1[c][:, :], w_hi[i][:, w], w_lo[i][:, w], x_hi[:, b, :], x_lo[:, b, :],
                            True, True).then_inc(l1_done, 1)

            def layer2(k, s):
                u, e, i, b = unit(k, s)
                if s % 2 == 0:
                    pe.wait_ge(w_lo_done, 2 * e + 2)
                pe.wait_ge(h1_lo_done, MC * (u + 1))
                for m in range(MC):
                    if s >= 2:
                        pe.wait_ge(z2_done, MC * (u - 2) + m + 1)
                    for c in range(MC):
                        w = slice(W2_AT[c] + m * P, W2_AT[c] + (m + 1) * P)
                        last = product(ps2[b][m][:, :], w_hi[i][:, w], w_lo[i][:, w], h1_hi[b][:, c, :],
                                       h1_lo[b][:, c, :], c == 0, c == MC - 1)
                    last.then_inc(l2_done, 1)

            def layer3(k, s):
                u, e, i, b = unit(k, s)
                final = isinstance(k, int) and 4 * k + s >= UNITS - B
                for c in range(MC):
                    pe.wait_ge(h2_lo_done, MC * u + c + 1)
                    w = slice(W3_AT[c], W3_AT[c] + H)
                    last = product(acc[b][:, :], w_hi[i][:, w], w_lo[i][:, w], h2_hi[b][:, c, :],
                                   h2_lo[b][:, c, :], False, final and c == MC - 1)
                last.then_inc(l3_done, 1)

            def finish(b):
                for t in range(TB):
                    if t % (TB // 2) == 0:
                        pe.wait_ge(x1_done, 2 * b + t // (TB // 2) + 1)
                    cols = slice(t * P, (t + 1) * P)
                    half = t // (TB // 2)
                    at = t % (TB // 2) * P
                    last = mm(fin[2 * b + half][:, at:at + P], x1T[:, b, cols], mix[:, :], start=True, stop=True)
                    if t % (TB // 2) == TB // 2 - 1:
                        last.then_inc(fin_done, 1)

            pe.wait_ge(wg_ready, 1)
            pe.wait_ge(gr_in, 16)
            for b in range(B):
                mm(gbias_ps[:, b * E:(b + 1) * E], gr[:, b:b + 1].to_broadcast([G + 2, P]), gr[:, B:B + E], start=True, stop=True)
            for b in range(B):
                pe.wait_ge(x_in[b], 16)
                for t in range(TB):
                    cols = slice(t * P, (t + 1) * P)
                    n = b * TB + t
                    last = mm(gate_ps[:, n, :], xT[:, b, cols], wg_s[:, :], start=True, stop=True)
            last.then_inc(gate_done, 1)
            pe.wait_ge(x_lo_done, 1)
            layer1(0, 0)
            pe.wait_ge(x_lo_done, 2)
            layer1(0, 1)
            pe.wait_ge(cw_done, 1)
            nc.tensor.transpose(cwT_ps, cw[:, :, :].rearrange("p e t -> p (e t)"), ident).then_inc(cwT_done, 1)
            layer2(0, 0)
            pe.wait_ge(cw_rows_done, 1)
            pe.wait_ge(ident_done, 1)
            for b in range(B):
                mm(acc[b][:, :], ident_r[:, :], x_hi[:, b, :], start=True, stop=False)
                mm(acc[b][:, :], ident_r[:, :], x_lo[:, b, :], start=False, stop=False)
            with pe.Fori(0, LOOPS) as k:
                for s in range(1, 5):
                    layer1(k, s + 1)
                    layer2(k, s)
                    layer3(k, s - 1)
            layer1(LOOPS, 2)
            layer2(LOOPS, 1)
            layer3(LOOPS, 0)
            layer1(LOOPS, 3)
            layer2(LOOPS, 2)
            layer3(LOOPS, 1)
            layer2(LOOPS, 3)
            pe.wait_ge(bias3_done, 3)
            for b in range(B):
                mm(acc[b][:, :], b3_parts[:, :], cw_parts[:, b * S:(b + 1) * S], start=False, stop=False)
            layer3(LOOPS, 2)
            layer3(LOOPS, 3)
            pe.wait_ge(mix_done, 1)
            pe.wait_ge(h1_act, 2 * MC * UNITS)
            finish(0)
            pe.wait_ge(z2_done, MC * (UNITS - 1))
            finish(1)



def _small_operands(a):
    j = np.arange(P) // QD
    d = np.arange(P) % QD
    k = np.arange(QC)
    right = np.array([[1, 1, 1, 1], [-1, 1, -1, 1], [-1, 1, 1, -1], [-1, -1, 1, 1]])
    left = np.array([[0, -1, -1, -1], [1, 0, -1, 1], [1, 1, 0, -1], [1, -1, 1, 0]])
    parts = {
        "rms_w": a["L0_cond_rms_w"].reshape(P, 1),
        "wg_W": a["L0_cond_wg_W"],
        "q_right": a["L1_cond_q_right"][k[None, :] ^ j[:, None], d[:, None]],
        "q_left": a["cond_256"][:, d].T,
        "gate": a["L1_cond_spectral_gate"].reshape(QD)[d].reshape(P, 1),
        "rank": np.broadcast_to(np.arange(E, 0, -1), (P, E)),
        "right_sign": right[:, j].T,
        "left_sign": np.broadcast_to(left.reshape(1, -1), (P, QC * QC)),
        "channel": d[:, None] == np.arange(QD)[None, :],
        "ident": np.eye(P),
    }
    out = np.empty((P, SMALL_COLS), np.float32)
    for name, (lo, hi) in SMALL.items():
        out[:, lo:hi] = parts[name]
    return out


def kernel(**inputs):
    import concourse.bacc as _bacc
    from concourse.bass_utils import run_bass_kernel_spmd as _run

    a = {name: np.asarray(v) for name, v in inputs.items()}
    weights = np.empty((E, P, W_COLS), np.float32)
    weights[:, :, W1_AT:W1_AT + M] = a["L0_cond_W1"]
    for c in range(MC):
        weights[:, :, W2_AT[c]:W2_AT[c] + M] = a["L0_cond_W2"][:, c * P:(c + 1) * P]
        weights[:, :, W3_AT[c]:W3_AT[c] + H] = a["L0_cond_W3"][:, c * P:(c + 1) * P]
    biases = np.stack([a["L0_cond_b1"].reshape(E, MC, P), a["L0_cond_b2"].reshape(E, MC, P)], axis=1)
    gate_rows = np.ones((G + 2, B + E), np.float32)
    gate_rows[0:G, 0:B] = a["cond_256"].T
    gate_rows[0:G, B:] = a["L0_cond_gg_W"]
    gate_rows[G, B:] = a["L0_cond_wg_b"]
    gate_rows[G + 1, B:] = a["L0_cond_gg_b"]
    arrays = {
        "x": np.ascontiguousarray(a["x"]),
        "x_t": np.ascontiguousarray(a["x"].transpose(2, 0, 1)),
        "small": _small_operands(a),
        "gate_rows": gate_rows,
        "weights": weights,
        "biases": np.ascontiguousarray(biases.reshape(E, 2 * MC, P).transpose(0, 2, 1)),
        "b3": np.ascontiguousarray(a["L0_cond_b3"]),
    }
    nc = _bacc.Bacc("TRN2", target_bir_lowering=False, num_devices=1)
    args = [nc.dram_tensor(name, v.shape, F32, kind="ExternalInput").ap() for name, v in arrays.items()]
    out = nc.dram_tensor("out", (B, S, H), F32, kind="ExternalOutput").ap()
    moe_rotate(nc, *args, out)
    r = _run(nc, [arrays], core_ids=[0])
    return r.results[0]["out"]
```

```python
from contextlib import ExitStack

import numpy as np

import concourse.bass as bass
from concourse import mybir

F32 = mybir.dt.float32
F32R = mybir.dt.float32r
BF16 = mybir.dt.bfloat16
ACT = mybir.ActivationFunctionType
ALU = mybir.AluOpType
AX = mybir.AxisListType

P = 128
B, S, H = 2, 512, 128
E, M, G = 8, 256, 32
MC = M // P
TB = S // P
T = B * TB
QC = 4
QD = H // QC
UNITS = E * B
STACK = (0, 32, 64)
RMS_EPS = 1e-6
NORM_EPS = 1e-8
BELOW_ALL = -3.0e38

W1_AT = 0
W2_AT = [M, 2 * M]
W3_AT = [3 * M, 3 * M + H]
W_COLS = 3 * M + MC * H
W_HALF = W_COLS // 2
WARM_UP = 9

SMALL = {}
_at = 0
for _name, _width in (("rms_w", 1), ("wg_W", E), ("q_right", QC), ("q_left", 2), ("gate", 1), ("rank", E),
                      ("right_sign", QC), ("left_sign", QC * QC), ("channel", QD), ("ident", P)):
    SMALL[_name] = (_at, _at + _width)
    _at += _width
SMALL_COLS = _at


def moe_rotate(nc, x, x_t, small, gate_rows, weights, biases, b3, out):
    cw_dram = nc.dram_tensor("cw_dram", [E, T * P], F32, kind="Internal").ap()

    ctx = ExitStack()
    with ctx:
        def sb(name, shape, dt=F32):
            return ctx.enter_context(nc.sbuf_tensor(name, shape, dt))

        def pb(name):
            return ctx.enter_context(nc.psum_tensor(name, [P, 512], F32))

        def sem(name):
            return ctx.enter_context(nc.semaphore(name))

        xT = sb("xT", [P, B, S])
        x_hi = sb("x_hi", [P, B, S], F32R)
        x_lo = sb("x_lo", [P, B, S], F32R)
        x_tok = sb("x_tok", [P, T, H])
        x_sq = sb("x_sq", [P, T, H])
        zero = sb("zero", [P, 1], BF16)
        sm = sb("sm", [P, SMALL_COLS])
        gr = sb("gr", [B * (G + 2), 1 + B * E])
        b3_raw = sb("b3_raw", [P, H])
        b3_parts = sb("b3_parts", [P, H], F32R)
        cw_raw = sb("cw_raw", [P, T * P])
        cw_parts = sb("cw_parts", [P, T * P], F32R)
        w_raw = [sb(f"w_raw{i}", [P, W_COLS]) for i in range(2)]
        w_hi = [sb(f"w_hi{i}", [P, W_COLS], F32R) for i in range(2)]
        w_lo = [sb(f"w_lo{i}", [P, W_COLS], F32R) for i in range(2)]
        bias = [sb(f"bias{i}", [P, 2 * MC]) for i in range(2)]
        cw_all = [sb(f"cw_all{i}", [P, T * P]) for i in range(2)]
        h1 = sb("h1", [P, MC, S])
        h1_hi = [sb(f"h1_hi{b}", [P, MC, S], F32R) for b in range(B)]
        h1_lo = [sb(f"h1_lo{b}", [P, MC, S], F32R) for b in range(B)]
        z2 = sb("z2", [P, MC, S])
        h2_hi = [sb(f"h2_hi{b}", [P, MC, S], F32R) for b in range(B)]
        h2_lo = [sb(f"h2_lo{b}", [P, MC, S], F32R) for b in range(B)]
        unit0 = sb("unit0", [P, S])
        base = sb("base", [P, S])
        x1T = sb("x1T", [P, B, S])
        out_sb = sb("out_sb", [P, B, S])
        minus_half = sb("minus_half", [P, T])
        wg_s = sb("wg_s", [P, E])
        ssq = sb("ssq", [P, T])
        ms = sb("ms", [P, T])
        rinv = sb("rinv", [P, T])
        logit = sb("logit", [P, T, E])
        top = sb("top", [P, T])
        below = sb("below", [P, T, E])
        prob = sb("prob", [P, T, E])
        key = sb("key", [P, T, E])
        best = sb("best", [P, T])
        first = sb("first", [P, T, E])
        rest = sb("rest", [P, T, E])
        chosen = sb("chosen", [P, T, E])
        total = sb("total", [P, T])
        scale = sb("scale", [P, T])
        cw = sb("cw", [P, E, T])
        cw_rows = sb("cw_rows", [E * T, P])
        q_sq = sb("q_sq", [P, QC + 2])
        q_pair = sb("q_pair", [P, 3])
        q_sum = sb("q_sum", [P, 2])
        q_norm = sb("q_norm", [P, 2])
        q_scale = sb("q_scale", [P, 1])
        right = sb("right", [P, QC])
        turned = sb("turned", [P, QC, QC])
        turned2 = sb("turned2", [P, QC, 2])
        turned1 = sb("turned1", [P, QC])
        part_a = sb("part_a", [P, QC])
        part_b = sb("part_b", [P, QC])
        coef = sb("coef", [P, QC])
        rot = sb("rot", [P, QC, QD])
        mix = sb("mix", [P, P])

        ps1 = [pb(f"ps1_{c}") for c in range(MC)]
        ps2 = [[pb(f"ps2_{b}_{m}") for m in range(MC)] for b in range(B)]
        acc = [pb(f"acc{b}") for b in range(B)]
        gate_ps = acc[1][:, 0:T * E].rearrange("p (t e) -> p t e", e=E)
        gbias_ps = acc[1][:, T * E:T * E + B * E]
        cwT_ps = acc[1][0:E * T, P:2 * P]
        unit0_ps = acc[1]
        ps_unit1 = ps2[1]
        fin = [ps1[0], ps1[1], ps2[0][0], ps2[0][1]]

        def small_at(name):
            a, z = SMALL[name]
            return sm[:, a:z]

        rank_bc = small_at("rank").unsqueeze(1).to_broadcast([P, T, E])
        ident = small_at("ident")

        x_in = [sem(f"x_in{b}") for b in range(B)]
        x_tok_in = [sem(f"x_tok_in{b}") for b in range(B)]
        w1_0_in = sem("w1_0_in")
        w2_0_in = sem("w2_0_in")
        cw_half_in = sem("cw_half_in")
        small_in = sem("small_in")
        gr_in = sem("gr_in")
        b3_in = sem("b3_in")
        raw_in = [sem(f"raw_in{i}") for i in range(2)]
        bias_in = [sem(f"bias_in{i}") for i in range(2)]
        cw_in = [sem(f"cw_in{i}") for i in range(2)]
        cw_out = sem("cw_out")
        cw_raw_in = sem("cw_raw_in")
        bias3_done = sem("bias3_done")
        out_done = sem("out_done")
        zero_ready = sem("zero_ready")
        x_sq_1_done = sem("x_sq_1_done")
        zeroed = sem("zeroed")
        x_hi_done = sem("x_hi_done")
        x_lo_done = [sem(f"x_lo_done{b}") for b in range(B)]
        wg_ready = sem("wg_ready")
        gate_done = sem("gate_done")
        ms_done = sem("ms_done")
        rinv_done = sem("rinv_done")
        below_done = sem("below_done")
        rest_done = sem("rest_done")
        total_done = sem("total_done")
        prob_done = sem("prob_done")
        cw_done = sem("cw_done")
        cwT_done = sem("cwT_done")
        cw_rows_done = sem("cw_rows_done")
        w_hi_done = sem("w_hi_done")
        w1_hi_0_done = sem("w1_hi_0_done")
        w1_lo_0_done = sem("w1_lo_0_done")
        w_lo_pool_done = sem("w_lo_pool_done")
        w_lo_done = sem("w_lo_done")
        l1_done = sem("l1_done")
        h1_act = sem("h1_act")
        h1_lo_0_done = sem("h1_lo_0_done")
        h1_lo_1_done = sem("h1_lo_1_done")
        h1_lo_done = sem("h1_lo_done")
        l2_done = sem("l2_done")
        z2_done = sem("z2_done")
        h2_hi_done = sem("h2_hi_done")
        h2_lo_done = sem("h2_lo_done")
        l3_done = sem("l3_done")
        unit0_out = sem("unit0_out")
        unit0_weighted = sem("unit0_weighted")
        base_done = sem("base_done")
        mix_done = sem("mix_done")
        x1_done = sem("x1_done")
        fin_done = sem("fin_done")
        out_ready = sem("out_ready")
        dve_order = sem("dve_order")
        pool_order = sem("pool_order")

        tokens = x.rearrange("b (t p) h -> p (b t) h", p=P)

        block = ctx.enter_context(nc.Block())

        LOOPS = 3

        def unit(k, s):
            return 4 * k + s, 2 * k + s // 2, (s // 2) % 2, s % 2

        @block.sync
        def _(sp):
            sp.dma_start(xT[:, 0, :], x_t[:, 0, :]).then_inc(x_in[0], 16)
            sp.dma_start(sm[:, :], small).then_inc(small_in, 16)
            sp.dma_start(x_tok[:, 0:TB, :], tokens[:, 0:TB, :]).then_inc(x_tok_in[0], 16)
            sp.dma_start(x_tok[:, TB:T, :], tokens[:, TB:T, :]).then_inc(x_tok_in[1], 16)
            sp.dma_start(bias[0][:, :], biases[0]).then_inc(bias_in[0], 16)
            sp.dma_start(xT[:, 1, :], x_t[:, 1, :]).then_inc(x_in[1], 16)
            sp.dma_start(w_raw[0][:, M:W_HALF], weights[0, :, M:W_HALF]).then_inc(w2_0_in, 16)
            sp.dma_start(gr[:, :], gate_rows).then_inc(gr_in, 16)
            sp.dma_start(w_raw[0][:, W_HALF:], weights[0, :, W_HALF:]).then_inc(raw_in[0], 16)
            sp.dma_start(w_raw[1][:, :], weights[1]).then_inc(raw_in[1], 16)
            sp.dma_start(bias[1][:, :], biases[1]).then_inc(bias_in[1], 16)
            sp.wait_ge(zeroed, 2)
            for row in STACK:
                sp.dma_start(b3_raw[row:row + E, :], b3).then_inc(b3_in, 16)
            sp.wait_ge(w_lo_pool_done, 1)
            sp.wait_ge(w_lo_done, 1)
            sp.dma_start(w_raw[0][:, :], weights[2]).then_inc(raw_in[0], 16)
            sp.wait_ge(cw_rows_done, 1)
            sp.dma_start(cw_dram.rearrange("e (t p) -> (e t) p", p=P), cw_rows[:, :]).then_inc(cw_out, 16)
            sp.wait_ge(cw_out, 16)
            sp.dma_start(cw_all[0][:, S:], cw_dram[0:1, S:].to_broadcast([P, S])).then_inc(cw_half_in, 16)
            sp.dma_start(cw_all[0][:, 0:S], cw_dram[0:1, 0:S].to_broadcast([P, S])).then_inc(cw_in[0], 16)
            sp.dma_start(cw_all[1][:, :], cw_dram[1:2, :].to_broadcast([P, T * P])).then_inc(cw_in[1], 16)
            sp.wait_ge(w_lo_pool_done, 2)
            sp.wait_ge(w_lo_done, 2)
            sp.dma_start(w_raw[1][:, :], weights[3]).then_inc(raw_in[1], 16)
            for row in STACK:
                sp.dma_start(cw_raw[row:row + E, :], cw_dram).then_inc(cw_raw_in, 16)

            def load_scales(e, i, z2_count):
                sp.wait_ge(z2_done, z2_count)
                sp.dma_start(cw_all[i][:, :], cw_dram[bass.ds(e, 1), :].to_broadcast([P, T * P])).then_inc(cw_in[i], 16)
                sp.dma_start(bias[i][:, :], biases[bass.ds(e, 1), :, :].rearrange("a p c -> (a p) c")).then_inc(bias_in[i], 16)

            sp.wait_ge(unit0_weighted, 1)
            with sp.Fori(0, E // 2 - 2) as k:
                for i in range(2):
                    e = 2 * k + i + 2
                    load_scales(e, i, 2 * MC * (e - 1))
                    sp.wait_ge(w_lo_done, 2 * e)
                    sp.dma_start(w_raw[i][:, :], weights[bass.ds(e + 2, 1), :, :].rearrange("a p c -> (a p) c")).then_inc(raw_in[i], 16)
            for i in range(2):
                e = E - 2 + i
                load_scales(e, i, 2 * MC * (e - 1))
            for b in range(B):
                rows = out[b].rearrange("(t p) h -> p t h", p=P)
                for h in range(2):
                    t = slice(h * TB // 2, (h + 1) * TB // 2)
                    sp.wait_ge(out_ready, 2 * b + h + 1)
                    sp.dma_start(rows[:, t, :], out_sb[:, b, :].rearrange("p (t h) -> p t h", h=H)[:, t, :]).then_inc(out_done, 16)
            sp.wait_ge(out_done, 16 * 2 * B)

        @block.gpsimd
        def _(pool):
            count = [0]

            def then(ins):
                ins.then_inc(pool_order, 1)
                count[0] += 1
                pool.wait_ge(pool_order, count[0])

            tt = nc.gpsimd.tensor_tensor
            nc.gpsimd.memset(zero[:, :], 0.0).then_inc(zero_ready, 1)
            then(nc.gpsimd.memset(minus_half[:, :], -0.5))
            nc.gpsimd.memset(b3_raw[:, :], 0.0).then_inc(zeroed, 1)
            nc.gpsimd.memset(cw_raw[:, :], 0.0).then_inc(zeroed, 1)
            pool.wait_ge(small_in, 16)
            nc.gpsimd.tensor_scalar(wg_s[:, :], small_at("wg_W"), small_at("rms_w"), 1.0, ALU.mult, ALU.mult).then_inc(wg_ready, 1)
            for b in range(B):
                row = slice(b * TB, (b + 1) * TB)
                pool.wait_ge(ms_done, b + 1)
                tt(rinv[:, row], ms[:, row], minus_half[:, row], ALU.pow).then_inc(rinv_done, 1)
            pool.wait_ge(w_hi_done, 2)
            tt(w_lo[0][:, W_HALF:], w_raw[0][:, W_HALF:], w_hi[0][:, W_HALF:].bitcast(F32), ALU.subtract).then_inc(w_lo_pool_done, 1)
            pool.wait_ge(w_hi_done, 3)
            tt(w_lo[1][:, 0:W_HALF], w_raw[1][:, 0:W_HALF], w_hi[1][:, 0:W_HALF].bitcast(F32), ALU.subtract).then_inc(w_lo_pool_done, 1)
            for c in range(MC):
                pool.wait_ge(h1_act, 2 * (MC + c + 1))
                tt(h1_lo[1][:, c, :], h1[:, c, :], h1_hi[1][:, c, :].bitcast(F32), ALU.subtract).then_inc(h1_lo_1_done, 1)

            qr, ql = small_at("q_right"), small_at("q_left")
            tt(q_sq[:, 0:QC], qr, qr, ALU.mult)
            then(tt(q_sq[:, QC:QC + 2], ql, ql, ALU.mult))
            then(tt(q_pair[:, :], q_sq[:, 0:QC + 2:2], q_sq[:, 1:QC + 2:2], ALU.add))
            tt(q_sum[:, 0:1], q_pair[:, 0:1], q_pair[:, 1:2], ALU.add)
            then(nc.gpsimd.tensor_copy(q_sum[:, 1:2], q_pair[:, 2:3]))
            then(nc.gpsimd.tensor_scalar(q_sum[:, :], q_sum[:, :], NORM_EPS, 1.0, ALU.add, ALU.mult))
            then(tt(q_norm[:, :], q_sum[:, :], minus_half[:, 0:2], ALU.pow))
            then(tt(q_scale[:, :], q_norm[:, 0:1], q_norm[:, 1:2], ALU.mult))
            then(tt(q_scale[:, :], q_scale[:, :], small_at("gate"), ALU.mult))
            then(tt(right[:, :], qr, small_at("right_sign"), ALU.mult))
            then(tt(turned[:, :, :], small_at("left_sign").rearrange("p (i k) -> p i k", k=QC),
                    right[:, :].unsqueeze(1).to_broadcast([P, QC, QC]), ALU.mult))
            then(tt(turned2[:, :, :], turned[:, :, 0:2], turned[:, :, 2:4], ALU.add))
            then(tt(turned1[:, :], turned2[:, :, 0], turned2[:, :, 1], ALU.add))
            nc.gpsimd.tensor_scalar(part_a[:, :], right[:, :], ql[:, 0:1], q_scale[:, 0:1], ALU.mult, ALU.mult)
            then(nc.gpsimd.tensor_scalar(part_b[:, :], turned1[:, :], ql[:, 1:2], q_scale[:, 0:1], ALU.mult, ALU.mult))
            then(tt(coef[:, :], part_a[:, :], part_b[:, :], ALU.add))
            then(tt(rot[:, :, :], small_at("channel").unsqueeze(1).to_broadcast([P, QC, QD]),
                    coef[:, :].unsqueeze(2).to_broadcast([P, QC, QD]), ALU.mult))
            tt(mix[:, :], rot[:, :, :].rearrange("p i d -> p (i d)"), ident, ALU.add).then_inc(mix_done, 1)

            pool.wait_ge(unit0_out, 1)
            pool.wait_ge(cw_in[0], 16)
            tt(base[:, :], unit0[:, :], cw_all[0][:, 0:S], ALU.mult).then_inc(unit0_weighted, 1)
            pool.wait_ge(unit0_weighted, 1)
            tt(base[:, :], base[:, :], xT[:, 0, :], ALU.add).then_inc(base_done, 1)

            lo_b3, lo_cw = slice(STACK[1], STACK[1] + E), slice(STACK[2], STACK[2] + E)
            pool.wait_ge(b3_in, 16 * len(STACK))
            then(nc.gpsimd.tensor_copy(b3_parts[:, :], b3_raw[:, :]))
            tt(b3_parts[lo_b3, :], b3_raw[lo_b3, :], b3_parts[lo_b3, :].bitcast(F32), ALU.subtract).then_inc(bias3_done, 1)
            pool.wait_ge(cw_raw_in, 16 * len(STACK))
            for b in range(B):
                cols = slice(b * S, (b + 1) * S)
                pool.wait_ge(bias3_done, b + 1)
                then(nc.gpsimd.tensor_copy(cw_parts[:, cols], cw_raw[:, cols]))
                tt(cw_parts[lo_cw, cols], cw_raw[lo_cw, cols], cw_parts[lo_cw, cols].bitcast(F32), ALU.subtract).then_inc(bias3_done, 1)

        @block.scalar
        def _(act):
            fn = nc.scalar.activation

            def split_hi(k, s, half):
                _, e, i, _ = unit(k, s)
                cols = slice(half * W_HALF, (half + 1) * W_HALF)
                act.wait_ge(raw_in[i], 16 * (k + s // 4 + 1))
                if half == 0 and s >= 4:
                    act.wait_ge(l2_done, MC * B * (e - 1))
                if half == 1 and s >= 2:
                    act.wait_ge(l1_done, MC * B * e + 1)
                fn(w_hi[i][:, cols], w_raw[i][:, cols], ACT.Copy).then_inc(w_hi_done, 1)

            def layer1_out(k, s, chunks=range(MC)):
                u, e, i, b = unit(k, s)
                ps = ps_unit1 if s == 1 else ps1
                if s % 2 == 0:
                    act.wait_ge(bias_in[i], 16 * (k + s // 4 + 1))
                for c in chunks:
                    act.wait_ge(l1_done, MC * u + c + 1)
                    if s == 1:
                        act.wait_ge(h1_lo_0_done, c + 1)
                    elif s == 2:
                        act.wait_ge(h1_lo_1_done, c + 1)
                    elif s >= 3:
                        act.wait_ge(h1_lo_done, MC * (u - 3) + c + 1)
                    fn(h1[:, c, :], ps[c][:, :], ACT.Relu, bias=bias[i][:, c:c + 1]).then_inc(h1_act, 1)
                    if s >= 2:
                        act.wait_ge(l2_done, MC * (u - 1))
                    fn(h1_hi[b][:, c, :], ps[c][:, :], ACT.Relu, bias=bias[i][:, c:c + 1]).then_inc(h1_act, 1)

            def layer2_out(k, s, m):
                u, e, i, b = unit(k, s)
                act.wait_ge(z2_done, MC * u + m + 1)
                if s >= 2 and m == 0:
                    act.wait_ge(l3_done, u - 1)
                fn(h2_hi[b][:, m, :], z2[:, m, :], ACT.Relu).then_inc(h2_hi_done, 1)

            def step(k, s):
                split = not (isinstance(k, int) and 4 * k + s + 2 >= UNITS)
                if split:
                    split_hi(k, (s // 2 + 1) * 2, s % 2)
                if not (isinstance(k, int) and 4 * k + s + 1 >= UNITS):
                    layer1_out(k, s + 1, range(1, MC))
                for m in range(MC):
                    layer2_out(k, s, m)
                if not (isinstance(k, int) and 4 * k + s + 2 >= UNITS):
                    layer1_out(k, s + 2, range(0, 1))

            act.dma_start(w_raw[0][:, 0:M], weights[0, :, 0:M]).then_inc(w1_0_in, 16)
            act.wait_ge(x_in[0], 16)
            fn(x_hi[:, 0, :], xT[:, 0, :], ACT.Copy).then_inc(x_hi_done, 1)
            act.wait_ge(w1_0_in, 16)
            fn(w_hi[0][:, 0:M], w_raw[0][:, 0:M], ACT.Copy).then_inc(w1_hi_0_done, 1)
            act.wait_ge(x_tok_in[1], 16)
            fn(x_sq[:, TB:T, :], x_tok[:, TB:T, :], ACT.Square).then_inc(x_sq_1_done, 1)
            act.wait_ge(bias_in[0], 16)
            act.wait_ge(l1_done, 1)
            fn(h1[:, 0, :], ps1[0][:, :], ACT.Relu, bias=bias[0][:, 0:1]).then_inc(h1_act, 1)
            act.wait_ge(x_in[1], 16)
            fn(x_hi[:, 1, :], xT[:, 1, :], ACT.Copy).then_inc(x_hi_done, 1)
            fn(h1_hi[0][:, 0, :], ps1[0][:, :], ACT.Relu, bias=bias[0][:, 0:1]).then_inc(h1_act, 1)
            act.wait_ge(w2_0_in, 16)
            fn(w_hi[0][:, M:W_HALF], w_raw[0][:, M:W_HALF], ACT.Copy).then_inc(w_hi_done, 1)
            split_hi(0, 0, 1)
            layer1_out(0, 0, range(1, MC))
            split_hi(0, 2, 0)
            layer1_out(0, 1, range(0, 1))
            act.wait_ge(below_done, 1)
            fn(prob[:, :, :], below[:, :, :], ACT.Exp).then_inc(prob_done, 1)
            layer1_out(0, 1, range(1, MC))
            act.wait_ge(cwT_done, 1)
            fn(cw_rows[:, :], cwT_ps, ACT.Copy).then_inc(cw_rows_done, 1)
            split_hi(0, 2, 1)
            for m in range(MC):
                layer2_out(0, 0, m)
            layer1_out(0, 2)
            act.wait_ge(l3_done, 1)
            fn(unit0[:, :], unit0_ps[:, :], ACT.Copy).then_inc(unit0_out, 1)
            layer1_out(0, 3, range(0, 1))
            for m in range(MC):
                layer2_out(0, 1, m)
            with act.Fori(0, LOOPS) as k:
                for s in range(2, 6):
                    step(k, s)
            for s in range(2, 4):
                step(LOOPS, s)
            for b in range(B):
                for h in range(2):
                    cols = slice(h * S // 2, (h + 1) * S // 2)
                    act.wait_ge(fin_done, 2 * b + h + 1)
                    fn(out_sb[:, b, cols], fin[2 * b + h][:, 0:S // 2], ACT.Copy).then_inc(out_ready, 1)

        @block.vector
        def _(dve):
            count = [0]

            def then(ins, steps=1):
                ins.then_inc(dve_order, 1)
                count[0] += steps
                dve.wait_ge(dve_order, count[0])

            tt, stt = nc.vector.tensor_tensor, nc.vector.scalar_tensor_tensor

            def bc(row):
                return row[:, :].unsqueeze(2).to_broadcast([P, T, E])

            def split_lo(k, s, half):
                _, e, i, _ = unit(k, s)
                cols = slice(half * W_HALF, (half + 1) * W_HALF)
                dve.wait_ge(w_hi_done, 2 * e + half + 1)
                tt(w_lo[i][:, cols], w_raw[i][:, cols], w_hi[i][:, cols].bitcast(F32), ALU.subtract).then_inc(w_lo_done, 1)

            def layer1_low(k, s, c):
                u, e, i, b = unit(k, s)
                dve.wait_ge(h1_act, 2 * (MC * u + c + 1))
                tt(h1_lo[b][:, c, :], h1[:, c, :], h1_hi[b][:, c, :].bitcast(F32), ALU.subtract).then_inc(
                    h1_lo_0_done if s == 0 else h1_lo_done, 1)

            def layer2_scale(k, s, m):
                u, e, i, b = unit(k, s)
                if m == 0:
                    if s % 2 == 0:
                        dve.wait_ge(bias_in[i], 16 * (k + s // 4 + 1))
                    if s == 1:
                        dve.wait_ge(cw_half_in, 16)
                    elif s >= 2:
                        dve.wait_ge(cw_in[i], 16 * (k + s // 4 + 1))
                dve.wait_ge(l2_done, MC * u + m + 1)
                if s >= 1:
                    dve.wait_ge(h2_lo_done, MC * u)
                b2 = bias[i][:, MC + m:MC + m + 1]
                if s == 0:
                    nc.vector.tensor_scalar(z2[:, m, :], ps2[b][m][:, :], b2, 0.0, ALU.add, ALU.max).then_inc(z2_done, 1)
                else:
                    stt(z2[:, m, :], ps2[b][m][:, :], b2, cw_all[i][:, b * S:(b + 1) * S], ALU.add, ALU.mult).then_inc(z2_done, 1)

            def layer2_low(k, s, m, n):
                u, e, i, b = unit(k, s)
                dve.wait_ge(h2_hi_done, MC * u + m + n)
                stt(h2_lo[b][:, m:m + n, :], z2[:, m:m + n, :], 0.0, h2_hi[b][:, m:m + n, :].bitcast(F32),
                    ALU.max, ALU.subtract).then_inc(h2_lo_done, n)

            def step(k, s):
                split = not (isinstance(k, int) and 4 * k + s + 2 >= UNITS)
                if split:
                    split_lo(k, (s // 2 + 1) * 2, s % 2)
                layer2_scale(k, s, 0)
                layer1_low(k, s + 1, 1)
                layer2_scale(k, s, 1)
                layer2_low(k, s, 0, MC)
                layer1_low(k, s + 2, 0)

            dve.wait_ge(x_hi_done, 1)
            tt(x_lo[:, 0, :], xT[:, 0, :], x_hi[:, 0, :].bitcast(F32), ALU.subtract).then_inc(x_lo_done[0], 1)
            dve.wait_ge(w1_hi_0_done, 1)
            tt(w_lo[0][:, 0:M], w_raw[0][:, 0:M], w_hi[0][:, 0:M].bitcast(F32), ALU.subtract).then_inc(w1_lo_0_done, 1)
            for b in range(B):
                row = slice(b * TB, (b + 1) * TB)
                if b == 0:
                    dve.wait_ge(x_tok_in[0], 16)
                    then(tt(x_sq[:, row, :], x_tok[:, row, :], x_tok[:, row, :], ALU.mult))
                else:
                    dve.wait_ge(x_sq_1_done, 1)
                then(nc.vector.tensor_reduce(ssq[:, row], x_sq[:, row, :], AX.X, ALU.add))
                nc.vector.tensor_scalar(ms[:, row], ssq[:, row], 1.0 / H, RMS_EPS, ALU.mult, ALU.add).then_inc(ms_done, 1)
            dve.wait_ge(x_hi_done, 2)
            tt(x_lo[:, 1, :], xT[:, 1, :], x_hi[:, 1, :].bitcast(F32), ALU.subtract).then_inc(x_lo_done[1], 1)
            layer1_low(0, 0, 0)
            dve.wait_ge(w_hi_done, 1)
            tt(w_lo[0][:, M:W_HALF], w_raw[0][:, M:W_HALF], w_hi[0][:, M:W_HALF].bitcast(F32), ALU.subtract).then_inc(w_lo_done, 1)
            dve.wait_ge(gate_done, 1)
            dve.wait_ge(rinv_done, B)
            then(tt(logit[:, :, :], gate_ps, bc(rinv), ALU.mult))
            l4 = logit[:, :, :].rearrange("p (b t) e -> p b t e", b=B)
            then(tt(l4, l4, gbias_ps.rearrange("p (b e) -> p b e", b=B).unsqueeze(2).to_broadcast([P, B, TB, E]), ALU.add))
            then(nc.vector.tensor_reduce(top[:, :], logit[:, :, :], AX.X, ALU.max))
            tt(below[:, :, :], logit[:, :, :], bc(top), ALU.subtract).then_inc(below_done, 1)
            dve.wait_ge(below_done, 1)
            layer1_low(0, 0, 1)
            then(stt(key[:, :, :], below[:, :, :], 0.0, rank_bc, ALU.is_ge, ALU.mult))
            then(nc.vector.tensor_reduce(best[:, :], key[:, :, :], AX.X, ALU.max))
            then(tt(first[:, :, :], rank_bc, bc(best), ALU.is_equal))
            stt(rest[:, :, :], first[:, :, :], BELOW_ALL, below[:, :, :], ALU.mult, ALU.add).then_inc(rest_done, 1)
            dve.wait_ge(prob_done, 1)
            nc.vector.tensor_reduce(total[:, :], prob[:, :, :], AX.X, ALU.add).then_inc(total_done, 1)
            dve.wait_ge(rest_done, 1)
            nc.vector.tensor_reduce(top[:, :], rest[:, :, :], AX.X, ALU.max).then_inc(rest_done, 1)
            dve.wait_ge(total_done, 1)
            nc.vector.reciprocal(scale[:, :], total[:, :]).then_inc(total_done, 1)
            dve.wait_ge(rest_done, 2)
            tt(rest[:, :, :], rest[:, :, :], bc(top), ALU.is_equal).then_inc(rest_done, 1)
            dve.wait_ge(total_done, 2)
            tt(prob[:, :, :], prob[:, :, :], bc(scale), ALU.mult).then_inc(total_done, 1)
            dve.wait_ge(rest_done, 3)
            then(tt(key[:, :, :], rest[:, :, :], rank_bc, ALU.mult))
            nc.vector.tensor_reduce(best[:, :], key[:, :, :], AX.X, ALU.max).then_inc(dve_order, 1)
            then(stt(rest[:, :, :], first[:, :, :], 2.0 * E, key[:, :, :], ALU.mult, ALU.add), 2)
            then(tt(chosen[:, :, :], rest[:, :, :], bc(best), ALU.is_ge))
            dve.wait_ge(total_done, 3)
            tt(cw[:, :, :].rearrange("p e t -> p t e"), prob[:, :, :], chosen[:, :, :], ALU.mult).then_inc(cw_done, 1)
            for m in range(MC):
                layer2_scale(0, 0, m)
            for m in range(MC):
                layer2_low(0, 0, m, 1)
            split_lo(0, 2, 1)
            for c in range(MC):
                layer1_low(0, 2, c)
            for m in range(MC):
                layer2_scale(0, 1, m)
            layer1_low(0, 3, 0)
            for m in range(MC):
                layer2_low(0, 1, m, 1)
            with dve.Fori(0, LOOPS) as k:
                for s in range(2, 6):
                    step(k, s)
            layer2_scale(LOOPS, 2, 0)
            layer1_low(LOOPS, 3, 1)
            layer2_scale(LOOPS, 2, 1)
            for m in range(MC):
                layer2_low(LOOPS, 2, m, 1)
            for m in range(MC):
                layer2_scale(LOOPS, 3, m)
            for m in range(MC):
                layer2_low(LOOPS, 3, m, 1)
            dve.wait_ge(l3_done, UNITS - 1)
            dve.wait_ge(base_done, 1)
            tt(x1T[:, 0, :], acc[0][:, :], base[:, :], ALU.add).then_inc(x1_done, 2)
            dve.wait_ge(l3_done, UNITS)
            for h in range(2):
                cols = slice(h * S // 2, (h + 1) * S // 2)
                tt(x1T[:, 1, cols], acc[1][:, cols], xT[:, 1, cols], ALU.add).then_inc(x1_done, 1)

        @block.tensor
        def _(pe):
            mm = nc.tensor.matmul

            def product(out_ps, hi_w, lo_w, hi_x, lo_x, start, stop):
                mm(out_ps, hi_w, hi_x, start=start, stop=False)
                mm(out_ps, hi_w, lo_x, start=False, stop=False)
                return mm(out_ps, lo_w, hi_x, start=False, stop=stop)

            def layer1(k, s, chunks=range(MC)):
                u, e, i, b = unit(k, s)
                ps = ps_unit1 if s == 1 else ps1
                if s == 2:
                    pe.wait_ge(w_lo_pool_done, 2)
                elif s >= 4 and s % 2 == 0:
                    pe.wait_ge(w_lo_done, 2 * e - 1)
                for c in chunks:
                    if s == 2:
                        pe.wait_ge(h1_act, 2 * (c + 1))
                    elif s >= 3:
                        pe.wait_ge(h1_act, 2 * (MC * (u - 1) + c + 1))
                    w = slice(W1_AT + c * P, W1_AT + (c + 1) * P)
                    product(ps[c][:, :], w_hi[i][:, w], w_lo[i][:, w], x_hi[:, b, :], x_lo[:, b, :],
                            True, True).then_inc(l1_done, 1)

            def layer2(k, s):
                u, e, i, b = unit(k, s)
                if s >= 2 and s % 2 == 0:
                    pe.wait_ge(w_lo_done, 2 * e)
                for m in range(MC):
                    if s >= 2:
                        pe.wait_ge(z2_done, MC * (u - 2) + m + 1)
                    for c in range(MC):
                        if m == 0:
                            if s == 1:
                                pe.wait_ge(h1_lo_1_done, c + 1)
                            else:
                                pe.wait_ge(h1_lo_done, MC * (u - 2) + c + 1)
                        w = slice(W2_AT[c] + m * P, W2_AT[c] + (m + 1) * P)
                        last = product(ps2[b][m][:, :], w_hi[i][:, w], w_lo[i][:, w], h1_hi[b][:, c, :],
                                       h1_lo[b][:, c, :], c == 0, c == MC - 1)
                    last.then_inc(l2_done, 1)

            def layer2_unit0():
                for c in range(MC):
                    pe.wait_ge(w_lo_pool_done if c else w_lo_done, 1)
                    pe.wait_ge(h1_lo_0_done, c + 1)
                    for m in range(MC):
                        w = slice(W2_AT[c] + m * P, W2_AT[c] + (m + 1) * P)
                        last = product(ps2[0][m][:, :], w_hi[0][:, w], w_lo[0][:, w], h1_hi[0][:, c, :],
                                       h1_lo[0][:, c, :], c == 0, c == MC - 1)
                        if c == MC - 1:
                            last.then_inc(l2_done, 1)

            def layer3(k, s):
                u, e, i, b = unit(k, s)
                opens = isinstance(k, int) and 4 * k + s < B
                final = isinstance(k, int) and (4 * k + s == 0 or 4 * k + s >= UNITS - B)
                ps = unit0_ps if opens and s == 0 else acc[b]
                for c in range(MC):
                    pe.wait_ge(h2_lo_done, MC * u + c + 1)
                    w = slice(W3_AT[c], W3_AT[c] + H)
                    last = product(ps[:, :], w_hi[i][:, w], w_lo[i][:, w], h2_hi[b][:, c, :],
                                   h2_lo[b][:, c, :], opens and c == 0, final and c == MC - 1)
                last.then_inc(l3_done, 1)

            def finish(b):
                for t in range(TB):
                    if t % (TB // 2) == 0:
                        pe.wait_ge(x1_done, 2 * b + t // (TB // 2) + 1)
                    cols = slice(t * P, (t + 1) * P)
                    half = t // (TB // 2)
                    at = t % (TB // 2) * P
                    last = mm(fin[2 * b + half][:, at:at + P], x1T[:, b, cols], mix[:, :], start=True, stop=True)
                    if t % (TB // 2) == TB // 2 - 1:
                        last.then_inc(fin_done, 1)

            def gate(b):
                for t in range(TB):
                    mm(gate_ps[:, b * TB + t, :], xT[:, b, t * P:(t + 1) * P], wg_s[:, :], start=True, stop=True)

            pe.wait_ge(zero_ready, 1)
            for n in range(WARM_UP):
                mm(acc[0][:, :], zero[:, :].to_broadcast([P, P]), zero[:, :].to_broadcast([P, S]), start=True, stop=n < WARM_UP - 1)
            w = slice(W1_AT, W1_AT + P)
            pe.wait_ge(w1_hi_0_done, 1)
            mm(ps1[0][:, :], w_hi[0][:, w], x_hi[:, 0, :], start=True, stop=False)
            pe.wait_ge(x_lo_done[0], 1)
            mm(ps1[0][:, :], w_hi[0][:, w], x_lo[:, 0, :], start=False, stop=False)
            pe.wait_ge(w1_lo_0_done, 1)
            mm(ps1[0][:, :], w_lo[0][:, w], x_hi[:, 0, :], start=False, stop=True).then_inc(l1_done, 1)
            layer1(0, 0, range(1, MC))
            pe.wait_ge(wg_ready, 1)
            gate(0)
            pe.wait_ge(x_in[1], 16)
            gate(1)
            pe.wait_ge(gr_in, 16)
            mm(gbias_ps, gr[:, 0:1].to_broadcast([B * (G + 2), P]), gr[:, 1:], start=True, stop=True).then_inc(gate_done, 1)
            pe.wait_ge(x_lo_done[1], 1)
            layer1(0, 1)
            layer2_unit0()
            layer1(0, 2)
            pe.wait_ge(cw_done, 1)
            nc.tensor.transpose(cwT_ps, cw[:, :, :].rearrange("p e t -> p (e t)"), ident).then_inc(cwT_done, 1)
            layer2(0, 1)
            pe.wait_ge(cw_rows_done, 1)
            layer3(0, 0)
            layer1(0, 3)
            layer2(0, 2)
            pe.wait_ge(unit0_out, 1)
            layer3(0, 1)
            with pe.Fori(0, LOOPS) as k:
                for s in range(3, 7):
                    layer1(k, s + 1)
                    layer2(k, s)
                    layer3(k, s - 1)
            layer2(LOOPS, 3)
            pe.wait_ge(bias3_done, 3)
            for b in range(B):
                mm(acc[b][:, :], b3_parts[:, :], cw_parts[:, b * S:(b + 1) * S], start=False, stop=False)
            layer3(LOOPS, 2)
            layer3(LOOPS, 3)
            pe.wait_ge(mix_done, 1)
            pe.wait_ge(h1_act, 2 * MC * UNITS)
            finish(0)
            pe.wait_ge(z2_done, MC * (UNITS - 1))
            finish(1)



def _small_operands(a):
    j = np.arange(P) // QD
    d = np.arange(P) % QD
    k = np.arange(QC)
    right = np.array([[1, 1, 1, 1], [-1, 1, -1, 1], [-1, 1, 1, -1], [-1, -1, 1, 1]])
    left = np.array([[0, -1, -1, -1], [1, 0, -1, 1], [1, 1, 0, -1], [1, -1, 1, 0]])
    parts = {
        "rms_w": a["L0_cond_rms_w"].reshape(P, 1),
        "wg_W": a["L0_cond_wg_W"],
        "q_right": a["L1_cond_q_right"][k[None, :] ^ j[:, None], d[:, None]],
        "q_left": a["cond_256"][:, d].T,
        "gate": a["L1_cond_spectral_gate"].reshape(QD)[d].reshape(P, 1),
        "rank": np.broadcast_to(np.arange(E, 0, -1), (P, E)),
        "right_sign": right[:, j].T,
        "left_sign": np.broadcast_to(left.reshape(1, -1), (P, QC * QC)),
        "channel": d[:, None] == np.arange(QD)[None, :],
        "ident": np.eye(P),
    }
    out = np.empty((P, SMALL_COLS), np.float32)
    for name, (lo, hi) in SMALL.items():
        out[:, lo:hi] = parts[name]
    return out


def kernel(**inputs):
    import concourse.bacc as _bacc
    from concourse.bass_utils import run_bass_kernel_spmd as _run

    a = {name: np.asarray(v) for name, v in inputs.items()}
    weights = np.empty((E, P, W_COLS), np.float32)
    weights[:, :, W1_AT:W1_AT + M] = a["L0_cond_W1"]
    for c in range(MC):
        weights[:, :, W2_AT[c]:W2_AT[c] + M] = a["L0_cond_W2"][:, c * P:(c + 1) * P]
        weights[:, :, W3_AT[c]:W3_AT[c] + H] = a["L0_cond_W3"][:, c * P:(c + 1) * P]
    biases = np.stack([a["L0_cond_b1"].reshape(E, MC, P), a["L0_cond_b2"].reshape(E, MC, P)], axis=1)
    gate_rows = np.zeros((B, G + 2, 1 + B * E), np.float32)
    gate_rows[:, :, 0] = 1.0
    for b in range(B):
        cols = slice(1 + b * E, 1 + (b + 1) * E)
        gate_rows[b, 0:G, 0] = a["cond_256"][b]
        gate_rows[b, 0:G, cols] = a["L0_cond_gg_W"]
        gate_rows[b, G, cols] = a["L0_cond_wg_b"]
        gate_rows[b, G + 1, cols] = a["L0_cond_gg_b"]
    arrays = {
        "x": np.ascontiguousarray(a["x"]),
        "x_t": np.ascontiguousarray(a["x"].transpose(2, 0, 1)),
        "small": _small_operands(a),
        "gate_rows": gate_rows.reshape(B * (G + 2), 1 + B * E),
        "weights": weights,
        "biases": np.ascontiguousarray(biases.reshape(E, 2 * MC, P).transpose(0, 2, 1)),
        "b3": np.ascontiguousarray(a["L0_cond_b3"]),
    }
    nc = _bacc.Bacc("TRN2", target_bir_lowering=False, num_devices=1)
    args = [nc.dram_tensor(name, v.shape, F32, kind="ExternalInput").ap() for name, v in arrays.items()]
    out = nc.dram_tensor("out", (B, S, H), F32, kind="ExternalOutput").ap()
    moe_rotate(nc, *args, out)
    r = _run(nc, [arrays], core_ids=[0])
    return r.results[0]["out"]
```
